# Optimizing a Trainium2 kernel written in Bass

```python
import numpy as np
import jax
import jax.numpy as jnp

def _softmax(x, axis=-1):
    return jax.nn.softmax(x, axis=axis)

def _gelu(x):
    return jax.nn.gelu(x, approximate=True)

def _silu(x):
    return jax.nn.silu(x)

def _sigmoid(x):
    return jax.nn.sigmoid(x)

def _layernorm(x, axis=-1, eps=1e-05):
    m = jnp.mean(x, axis=axis, keepdims=True)
    v = jnp.var(x, axis=axis, keepdims=True)
    return (x - m) / jnp.sqrt(v + eps)

def _scatter_add(tgt, idx, src, axis=0):
    return tgt.at[idx].add(src)

def _segment_sum(src, seg, n):
    return jax.ops.segment_sum(src, seg, n)
kernel_name = 'mk_lm_tower_d1_tok_ids1024_r4_3f8f19'

def setup_inputs(seed: int=0):
    np.random.seed(seed)
    _w = jnp.asarray

    def _rec_inputs():
        import jax
        import jax.numpy as jnp
        _rk = jax.random.key(seed)
        x = jax.random.randint(jax.random.fold_in(_rk, 1), (32, 512), 0, 31999, jnp.int32)
        return x
    x = _rec_inputs()

    def _L0_tok_setup():
        import math
        import jax, jax.numpy as jnp
        import numpy as np
        key = jax.random.key(seed)
        k1, k2, k3, k4 = jax.random.split(key, 4)
        B, S, V, D = (8, 512, 8000, 256)
        x = jax.random.randint(k1, (B, S), 0, V, dtype=jnp.int64)
        tok_table = jax.random.normal(k2, (V, D), dtype=jnp.float32)
        pos_table = jax.random.normal(k3, (S, D), dtype=jnp.float32)
        seg_table = jax.random.normal(k4, (2, D), dtype=jnp.float32)
        return {'x': x, 'sep_token': 102, 'tok_table': tok_table, 'pos_table': pos_table, 'seg_table': seg_table}
    _L0_tok_all = _L0_tok_setup()
    _L0_tok_in = {k: v for k, v in _L0_tok_all.items() if k in ('tok_table', 'pos_table', 'seg_table')}
    del _L0_tok_all

    def _L0_attn_setup():
        import jax, jax.numpy as jnp
        import numpy as np
        D_MODEL = 256
        N_HEADS = 16
        LATENT_HEADS = 8
        LATENT_DIM = 128
        N_LATENTS = 64
        WINDOW = 64
        HEAD_DIM = D_MODEL // N_HEADS
        LAT_HD = LATENT_DIM // LATENT_HEADS
        B, S = (2, 1024)

        def _pool_to_latents(x):
            Bx, Sx, C = x.shape
            chunk = max(1, Sx // N_LATENTS)
            return x.reshape(Bx, N_LATENTS, chunk, C).mean(axis=2)

        def _local_window_attn(Q, K, V):
            Bx, H, Sx, D = Q.shape
            W = WINDOW
            nb = Sx // W
            Qb = Q.reshape(Bx, H, nb, W, D)
            Kp = jnp.pad(K, ((0, 0), (0, 0), (W, 0), (0, 0))).reshape(Bx, H, nb + 1, W, D)
            Vp = jnp.pad(V, ((0, 0), (0, 0), (W, 0), (0, 0))).reshape(Bx, H, nb + 1, W, D)
            Kw = jnp.concatenate([Kp[:, :, :-1], Kp[:, :, 1:]], axis=3)
            Vw = jnp.concatenate([Vp[:, :, :-1], Vp[:, :, 1:]], axis=3)
            i = jnp.arange(W)[:, None]
            j = jnp.arange(2 * W)[None, :]
            base = (j > i) & (j <= i + W)
            blk0 = (jnp.arange(nb) > 0)[:, None, None] | (j >= W)[None, :, :]
            mask = base[None, :, :] & blk0
            sc = jnp.einsum('bhnid,bhnjd->bhnij', Qb, Kw) / np.sqrt(D).astype(np.float32)
            sc = jnp.where(mask[None, None], sc, -jnp.inf)
            p = jax.nn.softmax(sc, axis=-1)
            out = jnp.einsum('bhnij,bhnjd->bhnid', p, Vw)
            return out.reshape(Bx, H, Sx, D)
        key = jax.random.key(seed)
        ks = jax.random.split(key, 11)
        std = 0.02
        w = lambda k, shp: jax.random.normal(k, shp, jnp.float32) * std
        return {'x': jax.random.normal(ks[0], (B, S, D_MODEL), jnp.float32), 'wq': w(ks[1], (D_MODEL, D_MODEL)), 'wk': w(ks[2], (D_MODEL, D_MODEL)), 'wv': w(ks[3], (D_MODEL, D_MODEL)), 'wgq': w(ks[4], (D_MODEL, LATENT_DIM)), 'wgk': w(ks[5], (D_MODEL, LATENT_DIM)), 'wgv': w(ks[6], (D_MODEL, LATENT_DIM)), 'r_out_w': w(ks[7], (LATENT_DIM, D_MODEL)), 'gate_local_w': w(ks[8], (N_HEADS, HEAD_DIM)), 'gate_remote_w': w(ks[9], (N_HEADS, HEAD_DIM)), 'w_out': w(ks[10], (D_MODEL, D_MODEL))}
    _L0_attn_all = _L0_attn_setup()
    _L0_attn_in = {k: v for k, v in _L0_attn_all.items() if k in ('wq', 'wk', 'wv', 'wgq', 'wgk', 'wgv', 'r_out_w', 'gate_local_w', 'gate_remote_w', 'w_out')}
    del _L0_attn_all

    def _L0_ffn_setup():
        import jax, jax.numpy as jnp
        import numpy as np
        LN_EPS = 1e-05

        def layer_norm(x, g, b):
            mu = jnp.mean(x, axis=-1, keepdims=True)
            var = jnp.var(x, axis=-1, keepdims=True)
            return (x - mu) / jnp.sqrt(var + LN_EPS) * g + b

        def balanced_assignment(scores):
            T, E = scores.shape
            C = T // E
            taken = jnp.zeros((T,), dtype=bool)
            parts = []
            for e in range(E):
                s = jnp.where(taken, -jnp.inf, scores[:, e])
                _, idx = jax.lax.top_k(s, C)
                parts.append(idx)
                taken = taken.at[idx].set(True)
            return jnp.concatenate(parts)
        key = jax.random.key(seed)
        ks = jax.random.split(key, 4)
        B, S, D, F, E = (4, 512, 256, 1024, 8)
        return {'x': jax.random.normal(ks[0], (B, S, D), dtype=jnp.float32), 'centroids': jax.random.normal(ks[1], (E, D), dtype=jnp.float32) * 0.1, 'ln_g': jnp.ones((D,), dtype=jnp.float32), 'ln_b': jnp.zeros((D,), dtype=jnp.float32), 'w1': jax.random.normal(ks[2], (E, D, F), dtype=jnp.float32) * 0.02, 'b1': jnp.zeros((E, F), dtype=jnp.float32), 'w2': jax.random.normal(ks[3], (E, F, D), dtype=jnp.float32) * 0.02, 'b2': jnp.zeros((E, D), dtype=jnp.float32)}
    _L0_ffn_all = _L0_ffn_setup()
    _L0_ffn_in = {k: v for k, v in _L0_ffn_all.items() if k in ('centroids', 'ln_g', 'ln_b', 'w1', 'b1', 'w2', 'b2')}
    del _L0_ffn_all
    return {'x': x, 'L0_tok_tok_table': _L0_tok_in['tok_table'], 'L0_tok_pos_table': _L0_tok_in['pos_table'], 'L0_tok_seg_table': _L0_tok_in['seg_table'], 'L0_attn_wq': _L0_attn_in['wq'], 'L0_attn_wk': _L0_attn_in['wk'], 'L0_attn_wv': _L0_attn_in['wv'], 'L0_attn_wgq': _L0_attn_in['wgq'], 'L0_attn_wgk': _L0_attn_in['wgk'], 'L0_attn_wgv': _L0_attn_in['wgv'], 'L0_attn_r_out_w': _L0_attn_in['r_out_w'], 'L0_attn_gate_local_w': _L0_attn_in['gate_local_w'], 'L0_attn_gate_remote_w': _L0_attn_in['gate_remote_w'], 'L0_attn_w_out': _L0_attn_in['w_out'], 'L0_ffn_centroids': _L0_ffn_in['centroids'], 'L0_ffn_ln_g': _L0_ffn_in['ln_g'], 'L0_ffn_ln_b': _L0_ffn_in['ln_b'], 'L0_ffn_w1': _L0_ffn_in['w1'], 'L0_ffn_b1': _L0_ffn_in['b1'], 'L0_ffn_w2': _L0_ffn_in['w2'], 'L0_ffn_b2': _L0_ffn_in['b2']}

def reference(x, L0_tok_tok_table, L0_tok_pos_table, L0_tok_seg_table, L0_attn_wq, L0_attn_wk, L0_attn_wv, L0_attn_wgq, L0_attn_wgk, L0_attn_wgv, L0_attn_r_out_w, L0_attn_gate_local_w, L0_attn_gate_remote_w, L0_attn_w_out, L0_ffn_centroids, L0_ffn_ln_g, L0_ffn_ln_b, L0_ffn_w1, L0_ffn_b1, L0_ffn_w2, L0_ffn_b2):
    import jax
    import jax.numpy as jnp

    def _L0_tok_ref(x, sep_token, tok_table, pos_table, seg_table):
        import math
        import jax, jax.numpy as jnp
        import numpy as np
        B, S = x.shape
        D = tok_table.shape[1]
        seg = jax.lax.cummax((x == sep_token).astype(jnp.int32), axis=1)
        out = tok_table[x] + pos_table[jnp.arange(S)][None, :, :] + seg_table[seg]
        return out * jnp.asarray(math.sqrt(D), dtype=out.dtype)

    def _L0_attn_ref(x, wq, wk, wv, wgq, wgk, wgv, r_out_w, gate_local_w, gate_remote_w, w_out):
        import jax, jax.numpy as jnp
        import numpy as np
        D_MODEL = 256
        N_HEADS = 16
        LATENT_HEADS = 8
        LATENT_DIM = 128
        N_LATENTS = 64
        WINDOW = 64
        HEAD_DIM = D_MODEL // N_HEADS
        LAT_HD = LATENT_DIM // LATENT_HEADS
        B, S = (2, 1024)

        def _pool_to_latents(x):
            Bx, Sx, C = x.shape
            chunk = max(1, Sx // N_LATENTS)
            return x.reshape(Bx, N_LATENTS, chunk, C).mean(axis=2)

        def _local_window_attn(Q, K, V):
            Bx, H, Sx, D = Q.shape
            W = WINDOW
            nb = Sx // W
            Qb = Q.reshape(Bx, H, nb, W, D)
            Kp = jnp.pad(K, ((0, 0), (0, 0), (W, 0), (0, 0))).reshape(Bx, H, nb + 1, W, D)
            Vp = jnp.pad(V, ((0, 0), (0, 0), (W, 0), (0, 0))).reshape(Bx, H, nb + 1, W, D)
            Kw = jnp.concatenate([Kp[:, :, :-1], Kp[:, :, 1:]], axis=3)
            Vw = jnp.concatenate([Vp[:, :, :-1], Vp[:, :, 1:]], axis=3)
            i = jnp.arange(W)[:, None]
            j = jnp.arange(2 * W)[None, :]
            base = (j > i) & (j <= i + W)
            blk0 = (jnp.arange(nb) > 0)[:, None, None] | (j >= W)[None, :, :]
            mask = base[None, :, :] & blk0
            sc = jnp.einsum('bhnid,bhnjd->bhnij', Qb, Kw) / np.sqrt(D).astype(np.float32)
            sc = jnp.where(mask[None, None], sc, -jnp.inf)
            p = jax.nn.softmax(sc, axis=-1)
            out = jnp.einsum('bhnij,bhnjd->bhnid', p, Vw)
            return out.reshape(Bx, H, Sx, D)
        Bx, Sx, _ = x.shape
        chunk = max(1, Sx // N_LATENTS)
        Q = (x @ wq).reshape(Bx, Sx, N_HEADS, HEAD_DIM).transpose(0, 2, 1, 3)
        K = (x @ wk).reshape(Bx, Sx, N_HEADS, HEAD_DIM).transpose(0, 2, 1, 3)
        V = (x @ wv).reshape(Bx, Sx, N_HEADS, HEAD_DIM).transpose(0, 2, 1, 3)
        local = _local_window_attn(Q, K, V)
        GQ = (x @ wgq).reshape(Bx, Sx, LATENT_HEADS, LAT_HD).transpose(0, 2, 1, 3)
        GK = _pool_to_latents(x @ wgk).reshape(Bx, N_LATENTS, LATENT_HEADS, LAT_HD).transpose(0, 2, 1, 3)
        GV = _pool_to_latents(x @ wgv).reshape(Bx, N_LATENTS, LATENT_HEADS, LAT_HD).transpose(0, 2, 1, 3)
        lsc = jnp.einsum('bhsd,bhnd->bhsn', GQ, GK) / np.sqrt(LAT_HD).astype(np.float32)
        lmask = jnp.arange(N_LATENTS)[None, :] <= (jnp.arange(Sx) // chunk)[:, None]
        lsc = jnp.where(lmask[None, None], lsc, -jnp.inf)
        lp = jax.nn.softmax(lsc, axis=-1)
        rem = jnp.einsum('bhsn,bhnd->bhsd', lp, GV)
        rem = rem.transpose(0, 2, 1, 3).reshape(Bx, Sx, LATENT_DIM) @ r_out_w
        rem = rem.reshape(Bx, Sx, N_HEADS, HEAD_DIM).transpose(0, 2, 1, 3)
        gl = jax.nn.sigmoid(jnp.einsum('bhsd,hd->bhs', Q, gate_local_w))[..., None]
        gr = jax.nn.sigmoid(jnp.einsum('bhsd,hd->bhs', Q, gate_remote_w))[..., None]
        out = gl * local + gr * rem
        out = out.transpose(0, 2, 1, 3).reshape(Bx, Sx, D_MODEL)
        return out @ w_out

    def _L0_ffn_ref(x, centroids, ln_g, ln_b, w1, b1, w2, b2):
        import jax, jax.numpy as jnp
        import numpy as np
        LN_EPS = 1e-05

        def layer_norm(x, g, b):
            mu = jnp.mean(x, axis=-1, keepdims=True)
            var = jnp.var(x, axis=-1, keepdims=True)
            return (x - mu) / jnp.sqrt(var + LN_EPS) * g + b

        def balanced_assignment(scores):
            T, E = scores.shape
            C = T // E
            taken = jnp.zeros((T,), dtype=bool)
            parts = []
            for e in range(E):
                s = jnp.where(taken, -jnp.inf, scores[:, e])
                _, idx = jax.lax.top_k(s, C)
                parts.append(idx)
                taken = taken.at[idx].set(True)
            return jnp.concatenate(parts)
        D = x.shape[-1]
        feat = x.reshape(-1, D)
        T = feat.shape[0]
        E = centroids.shape[0]
        C = T // E
        norm = layer_norm(feat, ln_g, ln_b)
        scores = jax.lax.stop_gradient(norm @ centroids.T)
        sort_by_expert = balanced_assignment(scores)
        routed = feat[sort_by_expert].reshape(E, C, D)
        h = layer_norm(routed, ln_g, ln_b)
        h = jax.nn.gelu(jnp.einsum('ecd,edf->ecf', h, w1) + b1[:, None, :])
        h = jnp.einsum('ecf,efd->ecd', h, w2) + b2[:, None, :]
        out = routed + h
        inv = jnp.zeros((T,), dtype=jnp.int32).at[sort_by_expert].set(jnp.arange(T, dtype=jnp.int32))
        return out.reshape(T, D)[inv].reshape(x.shape)
    h = _L0_tok_ref(x, 102, L0_tok_tok_table, L0_tok_pos_table, L0_tok_seg_table)
    h = h + _L0_attn_ref(_layernorm(h, axis=-1), L0_attn_wq, L0_attn_wk, L0_attn_wv, L0_attn_wgq, L0_attn_wgk, L0_attn_wgv, L0_attn_r_out_w, L0_attn_gate_local_w, L0_attn_gate_remote_w, L0_attn_w_out)
    h = h + _L0_ffn_ref(_layernorm(h, axis=-1), L0_ffn_centroids, L0_ffn_ln_g, L0_ffn_ln_b, L0_ffn_w1, L0_ffn_b1, L0_ffn_w2, L0_ffn_b2)
    return h

_drawn_inputs = setup_inputs


def setup_inputs(seed=0):
    import zlib

    import numpy as np

    out = dict(_drawn_inputs(seed))
    spreads = {'L0_ffn_ln_g': (1.0, 0.6),
     'L0_ffn_ln_b': (0.0, 0.8),
     'L0_ffn_b1': (0.0, 0.8),
     'L0_ffn_b2': (0.0, 2.0)}
    factors = {'L0_attn_wq': 8.0,
     'L0_attn_wk': 8.0,
     'L0_attn_wv': 8.0,
     'L0_attn_wgq': 8.0,
     'L0_attn_wgk': 8.0,
     'L0_attn_wgv': 8.0,
     'L0_attn_r_out_w': 8.0,
     'L0_attn_gate_local_w': 8.0,
     'L0_attn_gate_remote_w': 8.0,
     'L0_attn_w_out': 8.0,
     'L0_ffn_centroids': 8.0,
     'L0_ffn_w1': 8.0,
     'L0_ffn_w2': 8.0}
    for name, (base, spread) in spreads.items():
        noise = np.random.default_rng([zlib.crc32(name.encode()), seed]).standard_normal(out[name].shape)
        drawn = base * np.exp(spread * noise) if base else spread * noise
        out[name] = jnp.asarray(drawn.astype(out[name].dtype))
    for name, factor in factors.items():
        out[name] = (out[name] * factor).astype(out[name].dtype)
    return out
```

```python
from contextlib import ExitStack

import numpy as np

import concourse.bass as bass
from concourse import mybir
from concourse.alu_op_type import AluOpType as ALU

F32 = mybir.dt.float32
BF16 = mybir.dt.bfloat16
I32 = mybir.dt.int32
U32 = mybir.dt.uint32
ACT = mybir.ActivationFunctionType
AX = mybir.AxisListType

P = 128
D = 256
KC = D // P
H = 16
HD = D // H
LH = 8
LD = LH * HD
NL = 64
W = 64
SEP = 102
EPS = 1e-5
NEG = -1e30
G = 4
NU = H // G + 1
BITS = 2
RADIX = 1 << BITS
DIGITS = 32 // BITS
TAKEN = -3e38
GT = 4
OW = HD + 1


def unit_head(g, n):
    return 2 * g + n % 2 + H // 2 * (n // 2)


def constants(S):
    i = np.arange(P)
    ident = np.eye(P, dtype=np.float32)
    ring = (i[:, None] - i[None, :]) % P < W
    first = ring & ~((i[:, None] < W) & (i[None, :] >= W))
    band = np.stack([np.where(m, 0.0, NEG) for m in (first, ring)], 1)
    tiles = S // P
    tok = np.arange(tiles)[None, :, None] * P + i[:, None, None]
    lat = np.where(np.arange(NL)[None, None, :] <= tok // (S // NL), 0.0, NEG)
    parity = np.stack([(i // HD) % 2 == 0, (i // HD) % 2 == 1], 1)
    own = (i[:, None] // HD == np.arange(LH)[None, :]) * (NL / S)
    before = i[:, None] < i[None, :]
    lane = np.broadcast_to(i[None, :], (P, P))
    f = lambda a: np.ascontiguousarray(a.reshape(P, -1).astype(np.float32))
    cols = [f(ident), f(band), f(lat), f(parity), f(own), f(before), f(lane), f(i)]
    digit = np.arange(1, RADIX, dtype=np.int64)[None, :] << (32 - BITS * (1 + np.arange(DIGITS, dtype=np.int64)))[:, None]
    digits = np.broadcast_to(digit.astype(np.uint32).view(np.int32).reshape(1, -1), (P, DIGITS * (RADIX - 1)))
    return np.concatenate(cols, 1), [c.shape[1] for c in cols], np.ascontiguousarray(digits)


def tower(nc, ins, out, cin, din, widths, SEQS, S, V, F, E):
    TS = S // P
    TOK = SEQS * S
    NT = TOK // P
    NUB = TS * NU
    C = TOK // E
    CT = C // P
    GR = CT // GT
    FC = F // P
    LC = min(8, NT // 8)
    LT = NT // LC
    assert S // NL * NL == S and TS == 4 and NT <= P and CT == GR * GT

    ctx = ExitStack()
    with ctx:
        def sb(name, shape, dt=F32):
            return ctx.enter_context(nc.sbuf_tensor(name, shape, dt))

        def sem(name):
            return ctx.enter_context(nc.semaphore(name))

        h1_rows = nc.dram_tensor("h1_rows", [TOK, D], F32, kind="Internal").ap()
        h1_tiles = h1_rows.rearrange("(n p) d -> p n d", p=P)

        S_ps = [ctx.enter_context(nc.psum_tensor(f"S_ps{j}", [P, 512], F32)) for j in range(2)]
        T_ps = [ctx.enter_context(nc.psum_tensor(f"T_ps{j}", [P, 512], F32)) for j in range(2)]
        O_ps = [ctx.enter_context(nc.psum_tensor(f"O_ps{j}", [P, 512], F32)) for j in range(2)]
        M_ps = [ctx.enter_context(nc.psum_tensor(f"M_ps{j}", [P, 512], F32)) for j in range(2)]

        cst = sb("cst", [P, sum(widths)])
        at = np.cumsum([0] + widths)
        c_ident, c_band, c_lat, c_parity, c_own, c_before, c_lane, c_part = (
            cst[:, int(at[n]):int(at[n + 1])] for n in range(len(widths)))
        identb = sb("identb", [P, P], BF16)
        band = sb("band", [P, 2, P], BF16)
        latm = sb("latm", [P, TS, NL], BF16)
        wq = sb("wq", [P, KC, D])
        wk = sb("wk", [P, KC, D])
        wvg = sb("wvg", [P, KC, D + 2 * H])
        wgq = sb("wgq", [P, KC, LD])
        wgk = sb("wgk", [P, KC, LD])
        wgv = sb("wgv", [P, KC, LD])
        wro = sb("wro", [P, D])
        wout = sb("wout", [P, KC, D])
        gates = sb("gates", [P, 2, D])
        gprod = sb("gprod", [P, KC, 2, D])
        cen = sb("cen", [E, D])
        cenT = sb("cenT", [P, KC, E])
        ln_rows = sb("ln_rows", [2 * KC, P])
        ln = sb("ln", [P, 2 * KC])
        lnb_row = sb("lnb_row", [P, KC, P])
        kb = sb("kb", [P, E])
        segs = sb("segs", [P, 2, D])
        P16 = sb("P16", [P, TS, D])
        D16 = sb("D16", [P, D])
        xi = sb("xi", [SEQS, S], I32)
        xf = sb("xf", [SEQS, S])
        xw = sb("xw", [SEQS, S])
        xs = sb("xs", [SEQS, S])
        idx_all = sb("idx_all", [P, TS, SEQS + 1], I32)
        seg_all = sb("seg_all", [P, TS, SEQS + 1])
        idx_now = sb("idx_now", [P, TS], I32)
        seg_now = sb("seg_now", [P, TS])
        rows = sb("rows", [P, TS, D])
        hres = sb("hres", [P, 2, TS, D])
        st0 = sb("st0", [P, 6])
        mv0 = sb("mv0", [P, TS, 2])
        ve0 = sb("ve0", [P, TS])
        rs0 = sb("rs0", [P, TS])
        mhalf = sb("mhalf", [P, 1])
        xn = sb("xn", [P, 2, D])
        x1T = sb("x1T", [P, KC, S])
        Qt = sb("Qt", [P, 2, S])
        Kt = [sb(f"Kt{j}", [P, 2, 1 + S // W, W]) for j in range(2)]
        Gt = sb("Gt", [P, S])
        Vo = sb("Vo", [P, TS, H, OW])
        Ve = sb("Ve", [P, TS + 1, H, OW])
        gt = sb("gt", [P, TS, 2 * H])
        xp = sb("xp", [P, KC, 2, NL])
        bdK = sb("bdK", [P, LH, NL])
        bdV = sb("bdV", [P, LH // 2, 2, OW])
        mx = sb("mx", [P, 2, LH])
        prob = sb("prob", [P, 2, 512])
        probT = [sb(f"probT{j}", [P, 512]) for j in range(2)]
        rc = sb("rc", [P, H + LH])
        rem = sb("rem", [P, LH, HD])
        sg = sb("sg", [P, 2 * H])
        cl = sb("cl", [P, H])
        loc = sb("loc", [P, H, HD])
        remT = sb("remT", [P, P])
        r2 = sb("r2", [P, H, HD])
        mix = sb("mix", [P, D])
        mixT = sb("mixT", [P, KC, P])
        h1 = sb("h1", [P, 2, D])
        st1 = sb("st1", [P, 6])
        mv1 = sb("mv1", [P, 2])
        ve1 = sb("ve1", [P, 1])
        rs1 = sb("rs1", [P, 1])
        y = sb("y", [P, D])
        yT = sb("yT", [P, KC, P])
        score = sb("score", [P, E, NT])

        digits = sb("digits", [P, DIGITS, RADIX - 1], I32)
        onesb = sb("onesb", [P, P], BF16)
        beforeb = sb("beforeb", [P, P], BF16)
        laneb = sb("laneb", [P, P], BF16)
        taken = sb("taken", [P, NT])
        zeros = sb("zeros", [P, NT])
        act_s = sb("act_s", [P, NT])
        thr = sb("thr", [P, 1], I32)
        cand = sb("cand", [P, RADIX - 1], I32)
        flip = sb("flip", [P, RADIX - 1], I32)
        cval = sb("cval", [P, RADIX - 1], I32)
        hits = sb("hits", [P, NT], BF16)
        counts = sb("counts", [P, RADIX - 1], BF16)
        over = sb("over", [P, RADIX - 1])
        nover = sb("nover", [P, 1])
        delta = sb("delta", [P, 1], U32)
        above = sb("above", [P, NT])
        equal = sb("equal", [P, NT], BF16)
        nabove = sb("nabove", [P, 1], BF16)
        need = sb("need", [P, 1])
        cum = sb("cum", [P, NT])
        rank = sb("rank", [P, NT])
        chosen = sb("chosen", [P, NT])
        chosenb = sb("chosenb", [P, NT], BF16)
        ranki = sb("ranki", [P, NT], I32)
        rlowi = sb("rlowi", [P, NT], I32)
        rlow = sb("rlow", [P, NT])
        rhigh = sb("rhigh", [P, NT], BF16)
        ohA = sb("ohA", [P, NT, CT], BF16)
        ohP = sb("ohP", [P, NT, CT], BF16)
        ohT = sb("ohT", [P, NT, CT], BF16)
        ohB = sb("ohB", [P, 2, LT, P], BF16)
        idx_next = sb("idx_next", [P, CT], I32)
        idx_cur = sb("idx_cur", [P, CT], I32)
        w1 = sb("w1", [P, KC, F])
        w2 = sb("w2", [P, FC, D])
        b1_rows = sb("b1_rows", [E * FC, P])
        b1_all = sb("b1_all", [P, E, FC])
        b1 = sb("b1", [P, FC])
        b2 = sb("b2", [P, D])
        hrow = sb("hrow", [P, 2, GT, D])
        st2 = sb("st2", [P, GT, 6])
        mv2 = sb("mv2", [P, GT, 2])
        ve2 = sb("ve2", [P, 2, GT])
        rs2 = sb("rs2", [P, 2, GT])
        r1 = sb("r1", [P, GT])
        nmr = sb("nmr", [P, GT])
        y2 = sb("y2", [P, 2, D])
        hT = [sb(f"hT{j}", [P, KC, GT * P]) for j in range(2)]
        hid = sb("hid", [P, FC, GT * P])
        orow = sb("orow", [P, 2, D])

        s_load = sem("s_load")
        s_cand = sem("s_cand")
        s_total = sem("s_total")
        s_cut = sem("s_cut")
        s_ties = sem("s_ties")
        s_sel = sem("s_sel")
        s_pos = sem("s_pos")
        s_ohA = sem("s_ohA")
        s_ohB = sem("s_ohB")
        s_used = sem("s_used")
        s_list = sem("s_list")
        s_next = sem("s_next")
        s_cur = sem("s_cur")
        s_gr = [sem(f"s_gr{q}") for q in range(GT)]
        s_var2 = sem("s_var2")
        s_rs2 = sem("s_rs2")
        s_y2 = sem("s_y2")
        s_yT = sem("s_yT")
        s_hT = sem("s_hT")
        s_l1 = sem("s_l1")
        s_hid = sem("s_hid")
        s_l2 = sem("s_l2")
        s_fin = sem("s_fin")
        s_add = sem("s_add")
        s_out = [sem(f"s_out{j}") for j in range(2)]
        s_free = sem("s_free")
        s_stand = sem("s_stand")
        s_w1 = sem("s_w1")
        s_w2 = sem("s_w2")
        s_b1 = sem("s_b1")
        s_b2 = sem("s_b2")
        s_init = sem("s_init")
        s_mh = sem("s_mh")
        s_setT = sem("s_setT")
        s_setE = sem("s_setE")
        s_idx = sem("s_idx")
        s_rows = [sem(f"s_rows{t}") for t in range(TS)]
        s_h0 = sem("s_h0")
        s_var0 = sem("s_var0")
        s_rs0 = sem("s_rs0")
        s_xn = sem("s_xn")
        s_x1T = sem("s_x1T")
        s_xp = sem("s_xp")
        s_misc = sem("s_misc")
        s_mA = sem("s_mA")
        s_mD = sem("s_mD")
        s_S = sem("s_S")
        s_shift = sem("s_shift")
        s_exp = sem("s_exp")
        s_T = sem("s_T")
        s_pT = sem("s_pT")
        s_PV = sem("s_PV")
        s_O = sem("s_O")
        s_rem = sem("s_rem")
        s_mix = sem("s_mix")
        s_h1out = [sem(f"s_h1out{j}") for j in range(2)]
        s_var1 = sem("s_var1")
        s_rs1 = sem("s_rs1")
        s_y = sem("s_y")
        s_v = sem("s_v")

        def stand(eng):
            eng.sem_inc(s_stand, 1)

        TAKER = {"ET": "A", "RT": "A", "RO": "D", "MT": "A", "WO": "D", "YT": "A", "SC": "D",
                 "Q": "A", "K": "D", "G": "A", "PK": "D", "PV": "D", "V": "A"}
        STEPS = NUB + 9
        plan = [[] for _ in range(STEPS)]
        for t in range(TS):
            for name, off in (("ET", 3), ("RT", 8), ("RO", 9), ("MT", 10), ("WO", 11), ("YT", 12), ("SC", 13)):
                plan[NU * t + off].append((name, t))
        proj = [[("Q", 0), ("Q", 1)], [("K", 0)], [("K", 1)], [("G", 0), ("PK", 0)], [("PV", 0)],
                [("V", 0)], [("V", 1), ("V", 2)], [("V", 3)]]
        for n, tasks in enumerate(proj):
            plan[NUB + n + (1 if n else 0)] += tasks
        head_tasks = [("ET", t) for t in range(TS)] + [x for step in proj for x in step]
        loop_tasks = [x for step in plan for x in step]

        class Misc:

            def __init__(self, tasks, b):
                before = {"A": 0, "D": 0}
                self.n0 = 0
                if b is not None:
                    self.n0 = len(head_tasks) + b * len(loop_tasks)
                    for e in before:
                        mine = lambda ts: sum(TAKER[x[0]] == e for x in ts)
                        before[e] = mine(head_tasks) + b * mine(loop_tasks)
                self.tasks, self.before = tasks, before

            def bank(self, task):
                return M_ps[self.tasks.index(task) % 2]

            def done(self, task):
                return self.n0 + self.tasks.index(task) + 1

            def free(self, eng, task):
                k = self.tasks.index(task) - 2
                if k >= 0:
                    e = TAKER[self.tasks[k][0]]
                    eng.wait_ge(s_mA if e == "A" else s_mD, self.out(self.tasks[k]))

            def out(self, task):
                e = TAKER[task[0]]
                k = self.tasks.index(task)
                return self.before[e] + sum(TAKER[x[0]] == e for x in self.tasks[:k + 1])

            def taken(self, e):
                return self.before[e]

        NCOPY = 3
        LOADS = 20
        block = ctx.enter_context(nc.Block())

        @block.sync
        def _(sp):
            v1 = lambda a: a.rearrange("(c p) -> c p", p=P)
            v2 = lambda a: a.rearrange("(c p) n -> p c n", p=P)
            loads = [
                (xi[:, :], ins["x"]), (cst[:, :], cin), (digits[:, :, :].rearrange("p a b -> p (a b)"), din),
                (b1_rows[:, :], ins["b1"].rearrange("e (m p) -> (e m) p", p=P)),
                (segs[:, 0, :], ins["seg_table"][0:1, :].to_broadcast([P, D])),
                (segs[:, 1, :], ins["seg_table"][1:2, :].to_broadcast([P, D])),
                (P16[:, :, :], ins["pos_table"].rearrange("(t p) d -> p t d", p=P)),
                (wq[:, :, :], v2(ins["wq"])), (wk[:, :, :], v2(ins["wk"])),
                (wvg[:, :, 0:D], v2(ins["wv"])), (wgq[:, :, :], v2(ins["wgq"])),
                (wgk[:, :, :], v2(ins["wgk"])), (wgv[:, :, :], v2(ins["wgv"])),
                (wro[:, :], ins["r_out_w"]), (wout[:, :, :], v2(ins["w_out"])),
                (gates[:, 0, :], ins["gate_local_w"].rearrange("(a h) d -> a (h d)", a=1).to_broadcast([P, D])),
                (gates[:, 1, :], ins["gate_remote_w"].rearrange("(a h) d -> a (h d)", a=1).to_broadcast([P, D])),
                (cen[:, :], ins["centroids"]),
                (ln_rows[0:KC, :], v1(ins["ln_g"])), (ln_rows[KC:2 * KC, :], v1(ins["ln_b"])),
            ]
            for dst, src in loads:
                sp.dma_start(dst, src).then_inc(s_load, 16)
            assert len(loads) == LOADS

            with sp.Fori(0, SEQS) as b:
                for t in range(TS):
                    sp.wait_ge(s_mD, Misc(loop_tasks, b).out(("WO", t)))
                    sp.dma_start(h1_tiles[:, bass.ds(TS * b + t, 1), :], h1[:, t % 2, :]).then_inc(s_h1out[t % 2], 16)
            sp.wait_ge(s_h1out[0], 16 * (NT // 2 + 1))
            sp.wait_ge(s_h1out[1], 16 * (NT // 2 + 1))
            w1_v = ins["w1"].rearrange("e (c p) f -> p e c f", p=P)
            w2_v = ins["w2"].rearrange("e (m p) d -> p e m d", p=P)
            sp.dma_start(w1[:, :, :], w1_v[:, 0, :, :]).then_inc(s_w1, 16)
            sp.dma_start(w2[:, :, :], w2_v[:, 0, :, :]).then_inc(s_w2, 16)
            sp.dma_start(b2[:, :], ins["b2"][0:1, :].to_broadcast([P, D])).then_inc(s_b2, 16)
            with sp.Fori(0, E - 1) as e:
                src1 = w1_v[:, bass.ds(e + 1, 1), :, :].rearrange("p a c f -> p (a c) f")
                src2 = w2_v[:, bass.ds(e + 1, 1), :, :].rearrange("p a m d -> p (a m) d")
                srcb = ins["b2"][bass.ds(e + 1, 1), :].to_broadcast([P, D])
                sp.wait_ge(s_l1, FC * GR * e + FC * GR)
                sp.dma_start(w1[:, :, :], src1).then_inc(s_w1, 16)
                sp.wait_ge(s_l2, CT * e + CT)
                sp.dma_start(w2[:, :, :], src2).then_inc(s_w2, 16)
                sp.wait_ge(s_add, CT * e + CT)
                sp.dma_start(b2[:, :], srcb).then_inc(s_b2, 16)

        def pool_embed(pool, bb, ready):
            def gather(t):
                if not isinstance(bb, int):
                    pool.wait_ge(s_h0, TS * bb + t - TS + 1)
                pool.wait_ge(s_idx, bb + 1)
                stand(pool)
                nc.gpsimd.indirect_dma_start(
                    rows[:, t, :], None, ins["tok_table"],
                    bass.IndirectOffsetOnAxis(idx_now[:, t:t + 1], 0)).then_inc(s_rows[t], 16)

            def power(t):
                pool.wait_ge(s_var0, TS * bb + t + 1)
                nc.gpsimd.tensor_tensor(out=rs0[:, t:t + 1], in0=ve0[:, t:t + 1], in1=mhalf[:, :],
                                        op=ALU.pow).then_inc(s_rs0, 1)
            return gather, power

        def pool_gather(pool, gi, q, idx, col):
            pool.wait_ge(s_fin, GT * gi if not isinstance(gi, int) else max(GT * gi, 1))
            stand(pool)
            half = (col // GT) % 2
            nc.gpsimd.indirect_dma_start(
                hrow[:, half, q, :], None, h1_rows,
                bass.IndirectOffsetOnAxis(idx[:, col:col + 1], 0)).then_inc(s_gr[q], 16)

        def pool_expert(pool, e, last):
            for g in range(GR):
                gi = GR * e + g
                if g + 1 < GR:
                    if g == 0:
                        pool.wait_ge(s_cur, e + 1)
                    for q in range(GT):
                        pool_gather(pool, gi + 1, q, idx_cur, (g + 1) * GT + q)
                elif not last:
                    pool.wait_ge(s_next, e + 2)
                    for q in range(GT):
                        pool_gather(pool, gi + 1, q, idx_next, q)
                if g + 1 < GR or not last:
                    pool_power(pool, gi + 1)
                for q in range(GT):
                    if (g, q) == (0, 0):
                        pool.wait_ge(s_b2, 16 * e + 16)
                    pool.wait_ge(s_fin, GT + GT * gi + q + 1)
                    nc.gpsimd.tensor_tensor(out=orow[:, q % 2, :], in0=orow[:, q % 2, :], in1=b2[:, :],
                                            op=ALU.add).then_inc(s_add, 1)
                    pool.wait_ge(s_add, GT * gi + q + 1)
                    stand(pool)
                    nc.gpsimd.indirect_dma_start(
                        out, bass.IndirectOffsetOnAxis(idx_cur[:, g * GT + q:g * GT + q + 1], 0),
                        orow[:, q % 2, :], None).then_inc(s_out[q % 2], 16)
                    done = ([q - 1] if q else []) + ([q] if q == GT - 1 else [])
                    for r in done:
                        pool.wait_ge(s_out[r % 2], 16 * (GT // 2 * gi + r // 2 + 1))
                    if done:
                        pool.sem_inc(s_free, len(done))

        def pool_power(pool, gi):
            pool.wait_ge(s_var2, gi + 1)
            nc.gpsimd.tensor_tensor(out=rs2[:, :, :], in0=ve2[:, :, :],
                                    in1=mhalf[:, :].unsqueeze(2).to_broadcast([P, 2, GT]), op=ALU.pow).then_inc(s_rs2, 1)

        @block.gpsimd
        def _(pool):
            nc.gpsimd.memset(mhalf[:, :], -0.5).then_inc(s_mh, 1)
            pool.wait_ge(s_mh, 1)
            gather, power = pool_embed(pool, 0, 1)
            for t in range(TS):
                gather(t)
            for t in range(TS):
                power(t)
            with pool.Fori(0, SEQS) as b:
                gather, power = pool_embed(pool, b + 1, 1)
                for t in range(TS):
                    gather(t)
                for s in range(STEPS):
                    for t in range(TS):
                        if s == NU * t + 1:
                            power(t)
                        if s == NU * t + 11:
                            pool.wait_ge(s_var1, TS * b + t + 1)
                            nc.gpsimd.tensor_tensor(out=rs1[:, :], in0=ve1[:, :], in1=mhalf[:, :],
                                                    op=ALU.pow).then_inc(s_rs1, 1)
            pool.wait_ge(s_h1out[0], 16 * (NT // 2 + 1))
            pool.wait_ge(s_h1out[1], 16 * (NT // 2 + 1))
            pool.wait_ge(s_next, 1)
            for q in range(GT):
                pool_gather(pool, 0, q, idx_next, q)
            pool_power(pool, 0)
            with pool.Fori(0, E - 1) as e:
                pool_expert(pool, e, False)
            pool_expert(pool, E - 1, True)
            for j in range(2):
                pool.wait_ge(s_out[j], 16 * (NT // 2))

        def act_misc(act, m, task, b):
            name, t = task
            if TAKER[name] != "A":
                return
            bank = m.bank(task)
            act.wait_ge(s_misc, m.done(task))
            if name == "ET":
                if t == 0 and b is not None:
                    act.wait_ge(s_xp, b + 1)
                nc.scalar.activation(x1T[:, :, t * P:(t + 1) * P],
                                     bank[:, 0:D].rearrange("p (c n) -> p c n", c=KC), ACT.Copy).then_inc(s_mA, 1)
            elif name == "RT":
                nc.scalar.activation(remT[:, :], bank[:, 0:P], ACT.Copy).then_inc(s_mA, 1)
            elif name == "MT":
                nc.scalar.activation(mixT[:, :, :], bank[:, 0:D].rearrange("p (c n) -> p c n", c=KC),
                                     ACT.Copy).then_inc(s_mA, 1)
            elif name == "YT":
                nc.scalar.activation(yT[:, :, :], bank[:, 0:D].rearrange("p (c n) -> p c n", c=KC),
                                     ACT.Copy).then_inc(s_mA, 1)
            elif name == "Q":
                nc.scalar.activation(Qt[:, t, :], bank[:, :], ACT.Copy, scale=HD ** -0.5).then_inc(s_mA, 1)
            elif name == "G":
                nc.scalar.activation(Gt[:, :], bank[:, :], ACT.Copy, scale=HD ** -0.5).then_inc(s_mA, 1)
            elif name == "V":
                v = bank[:, 0:D].rearrange("p (h d) -> p h d", h=H)
                nc.scalar.activation(Vo[:, t, :, 0:HD], v, ACT.Copy)
                nc.scalar.activation(Ve[0:W, t, :, 0:HD], v[0:W, :, :], ACT.Copy)
                nc.scalar.activation(Ve[W:P, t + 1, :, 0:HD], v[W:P, :, :], ACT.Copy)
                nc.scalar.activation(gt[:, t, :], bank[:, D:D + 2 * H], ACT.Tanh, scale=0.5).then_inc(s_mA, 1)

        def act_transposed(act, gi, q, g):
            act.wait_ge(s_yT, GT * gi + q + 1)
            for c in range(KC):
                ins_ = nc.scalar.activation(hT[g % 2][:, c, q * P:(q + 1) * P], T_ps[q % 2][:, c * P:(c + 1) * P],
                                            ACT.Identity, scale=ln[:, c:c + 1], bias=ln[:, KC + c:KC + c + 1])
            ins_.then_inc(s_hT, 1)

        def act_expert(act, e, last):
            for g in range(GR):
                gi = GR * e + g
                if g == 0:
                    act.wait_ge(s_b1, e + 1)
                for m in range(FC):
                    act.wait_ge(s_l1, FC * gi + m + 1)
                    nc.scalar.activation(hid[:, m, :], S_ps[m % 2][:, 0:GT * P], ACT.Gelu_apprx_tanh,
                                         bias=b1[:, m:m + 1]).then_inc(s_hid, 1)
                if g + 1 < GR or not last:
                    for q in range(GT):
                        act_transposed(act, gi + 1, q, g + 1 if g + 1 < GR else 0)

        @block.scalar
        def _(act):
            act.wait_ge(s_init, 3)
            nc.scalar.activation(probT[0][:, 0:P], c_ident, ACT.Copy).then_inc(s_pT, 2)
            m = Misc(head_tasks, None)
            for task in head_tasks:
                act_misc(act, m, task, None)
            with act.Fori(0, SEQS) as b:
                m = Misc(loop_tasks, b)
                for s in range(STEPS):
                    u = s - 1
                    if 0 <= u < NUB:
                        act.wait_ge(s_T, NUB * b + u + 1)
                        nc.scalar.activation(probT[u % 2][:, :], T_ps[u % 2][:, :], ACT.Copy).then_inc(s_pT, 1)
                    if s < NUB:
                        act.wait_ge(s_shift, 2 + NUB * b + s + 1)
                        nc.scalar.activation(prob[:, s % 2, :], prob[:, s % 2, :], ACT.Exp).then_inc(s_exp, 1)
                    for task in plan[s]:
                        act_misc(act, m, task, b)
            nc.scalar.activation(probT[0][:, 0:P], c_ident, ACT.Copy).then_inc(s_hid, 2)
            for q in range(GT):
                act_transposed(act, 0, q, 0)
            with act.Fori(0, E - 1) as e:
                act_expert(act, e, False)
            act_expert(act, E - 1, True)

        def pe_misc(pe, m, task, b):
            name, t = task
            if TAKER[name] is None:
                return
            bb = 0 if b is None else b + 1
            bank = m.bank(task)
            m.free(pe, task)
            if name == "ET":
                pe.wait_ge(s_xn, TS * bb + t + 1)
                for c in range(KC):
                    mm = nc.tensor.transpose(bank[:, c * P:(c + 1) * P], xn[:, t % 2, c * P:(c + 1) * P], c_ident)
            elif name == "RT":
                pe.wait_ge(s_rem, TS * b + t + 1)
                mm = nc.tensor.transpose(bank[:, 0:P], rem[:, :, :].rearrange("p h d -> p (h d)"), c_ident)
            elif name == "RO":
                pe.wait_ge(s_mA, m.out(("RT", t)))
                mm = nc.tensor.matmul(bank[:, 0:D], remT[:, :], wro[:, :], start=True, stop=True)
            elif name == "MT":
                pe.wait_ge(s_mix, TS * b + t + 1)
                for c in range(KC):
                    mm = nc.tensor.transpose(bank[:, c * P:(c + 1) * P], mix[:, c * P:(c + 1) * P], c_ident)
            elif name == "WO":
                pe.wait_ge(s_mA, m.out(("MT", t)))
                for c in range(KC):
                    mm = nc.tensor.matmul(bank[:, 0:D], mixT[:, c, :], wout[:, c, :], start=c == 0, stop=c == KC - 1)
            elif name == "YT":
                pe.wait_ge(s_y, TS * b + t + 1)
                for c in range(KC):
                    mm = nc.tensor.transpose(bank[:, c * P:(c + 1) * P], y[:, c * P:(c + 1) * P], c_ident)
            elif name == "SC":
                pe.wait_ge(s_mA, m.out(("YT", t)))
                for c in range(KC):
                    mm = nc.tensor.matmul(bank[:, 0:E], yT[:, c, :], cenT[:, c, :], start=c == 0, stop=c == KC - 1)
            elif name in "QKG":
                if (name, t) == ("Q", 0):
                    pe.wait_ge(s_mA, m.out(("ET", TS - 1)))
                w = {"Q": wq, "K": wk, "G": wgq}[name]
                for c in range(KC):
                    mm = nc.tensor.matmul(bank[:, :], w[:, c, t * P:(t + 1) * P], x1T[:, c, :],
                                          start=c == 0, stop=c == KC - 1)
            elif name == "PK":
                pe.wait_ge(s_xp, bb + 1)
                for c in range(KC):
                    mm = nc.tensor.matmul(bank[:, 0:NL], wgk[:, c, :], xp[:, c, 0, :], start=c == 0, stop=c == KC - 1)
            elif name == "PV":
                for c in range(KC):
                    mm = nc.tensor.matmul(bank[:, 0:LD], xp[:, c, :, :].rearrange("p a n -> p (a n)"), wgv[:, c, :],
                                          start=c == 0, stop=c == KC - 1)
            elif name == "V":
                for c in range(KC):
                    mm = nc.tensor.matmul(bank[:, 0:D + 2 * H], x1T[:, c, t * P:(t + 1) * P], wvg[:, c, :],
                                          start=c == 0, stop=c == KC - 1)
            mm.then_inc(s_misc, 1)

        LPS = M_ps[1][:, 0:CT]

        def pe_choice(pe, n, part, k):
            if part == "radix":
                pe.wait_ge(s_cand, DIGITS * n + k + 1)
                nc.tensor.matmul(M_ps[0][:, 0:RADIX - 1], onesb[:, :], counts[:, :], start=True, stop=True)\
                    .then_inc(s_total, 1)
            elif part == "ties":
                pe.wait_ge(s_cut, n + 1)
                nc.tensor.matmul(M_ps[0][:, 0:NT], beforeb[:, :], equal[:, :], start=True, stop=True)
                nc.tensor.matmul(M_ps[0][:, P:P + NT], onesb[:, :], equal[:, :], start=True, stop=True)
                nc.tensor.matmul(M_ps[0][:, 2 * P:2 * P + 1], onesb[:, :], nabove[:, :], start=True, stop=True)\
                    .then_inc(s_ties, 1)
            elif part == "pos":
                pe.wait_ge(s_sel, n + 1)
                nc.tensor.matmul(M_ps[0][:, 0:NT], beforeb[:, :], chosenb[:, :], start=True, stop=True)
                nc.tensor.matmul(M_ps[0][:, P:P + NT], onesb[:, :], chosenb[:, :], start=True, stop=True)\
                    .then_inc(s_pos, 1)
            elif part == "list":
                if k == 0:
                    pe.wait_ge(s_ohA, n + 1)
                pe.wait_ge(s_ohB, LC * n + k + 1)
                for j in range(LT):
                    for half in (ohP, ohT):
                        first_, last_ = k == 0 and j == 0 and half is ohP, k == LC - 1 and j == LT - 1 and half is ohT
                        mm = nc.tensor.matmul(LPS, ohB[:, k % 2, j, :], half[:, k * LT + j, :],
                                              start=first_, stop=last_)
                mm.then_inc(s_used, 1)

        CHOICE = {}
        slots = [(g, s) for g in range(GR) for s in range(FC + GT)]
        assert GR % 2 == 0
        if GR == 4:
            radix_at = [(g, s) for g in range(2) for s in [0, 2, 4, 6] + list(range(FC, FC + GT))]
            rest_at = {(2, 0): ["ties"], (2, 2): ["pos"]}
            lists_at = [(2, FC + q) for q in range(GT)] + [(3, m) for m in range(4)]
        else:
            radix_at = [(0, s) for s in range(8) for _ in range(2)]
            rest_at = {(0, 8): ["ties"], (0, 9): ["pos"]}
            lists_at = [(0, 10)] * 4 + [(1, 1)] * 4
        assert len(lists_at) >= LC and len(radix_at) == DIGITS
        for k, at_ in enumerate(radix_at):
            CHOICE.setdefault(at_, []).append(("radix", k))
        for at_, parts in rest_at.items():
            CHOICE.setdefault(at_, []).extend((x, 0) for x in parts)
        for k in range(LC):
            CHOICE.setdefault(lists_at[k], []).append(("list", k))
        ALL_PARTS = [("radix", k) for k in range(DIGITS)] + [("ties", 0), ("pos", 0)] + [("list", k) for k in range(LC)]
        STATS_AT = FC - 1

        def pe_rows(pe, gi, q):
            pe.wait_ge(s_y2, GT * gi + q + 1)
            if q >= 2:
                pe.wait_ge(s_hT, GT * gi + q - 1)
            else:
                pe.wait_ge(s_hid, 2)
            for c in range(KC):
                mm = nc.tensor.transpose(T_ps[q % 2][:, c * P:(c + 1) * P], y2[:, q % 2, c * P:(c + 1) * P], c_ident)
            mm.then_inc(s_yT, 1)

        def pe_expert(pe, e, last):
            for g in range(GR):
                gi = GR * e + g
                for m in range(FC):
                    if m == 0:
                        pe.wait_ge(s_hT, GT * gi + GT)
                        if g == 0:
                            pe.wait_ge(s_w1, 16 * e + 16)
                    pe.wait_ge(s_hid, FC * gi + m + 1)
                    for c in range(KC):
                        mm = nc.tensor.matmul(S_ps[m % 2][:, 0:GT * P], w1[:, c, m * P:(m + 1) * P], hT[g % 2][:, c, :],
                                              start=c == 0, stop=c == KC - 1)
                    mm.then_inc(s_l1, 1)
                    if not last:
                        for part, k in CHOICE.get((g, m), []):
                            pe_choice(pe, e + 1, part, k)
                for q in range(GT):
                    if g + 1 < GR or not last:
                        pe_rows(pe, gi + 1, q)
                    if q == 0:
                        pe.wait_ge(s_hid, 2 + FC * gi + FC)
                        if g == 0:
                            pe.wait_ge(s_w2, 16 * e + 16)
                    pe.wait_ge(s_fin, GT + GT * gi + q - 1)
                    for m in range(FC):
                        mm = nc.tensor.matmul(O_ps[q % 2][:, 0:D], hid[:, m, q * P:(q + 1) * P], w2[:, m, :],
                                              start=m == 0, stop=m == FC - 1)
                    mm.then_inc(s_l2, 1)
                    if not last:
                        for part, k in CHOICE.get((g, FC + q), []):
                            pe_choice(pe, e + 1, part, k)

        @block.tensor
        def _(pe):
            pe.wait_ge(s_load, 16 * LOADS)
            pe.wait_ge(s_init, 3)
            for t in range(TS):
                nc.tensor.transpose(M_ps[0][:, t * SEQS:(t + 1) * SEQS], xw[:, t * P:(t + 1) * P],
                                    c_ident[0:SEQS, 0:SEQS])
                nc.tensor.transpose(M_ps[0][:, (TS + t) * SEQS:(TS + t + 1) * SEQS], xs[:, t * P:(t + 1) * P],
                                    c_ident[0:SEQS, 0:SEQS])
            for c in range(KC):
                mm = nc.tensor.transpose(M_ps[1][:, c * E:(c + 1) * E], cen[:, c * P:(c + 1) * P], c_ident[0:E, 0:E])
            nc.tensor.transpose(M_ps[1][:, 128:128 + E * FC], b1_rows[:, :], c_ident[0:E * FC, 0:E * FC])
            mm = nc.tensor.transpose(M_ps[1][:, 32:32 + 2 * KC], ln_rows[:, :], c_ident[0:2 * KC, 0:2 * KC])
            mm.then_inc(s_setT, 1)
            pe.wait_ge(s_setE, 2)
            for c in range(KC):
                mm = nc.tensor.matmul(M_ps[1][:, 64:64 + E], lnb_row[:, c, :], cenT[:, c, :],
                                      start=c == 0, stop=c == KC - 1)
            mm.then_inc(s_setT, 1)
            pe.wait_ge(s_setE, 4)
            m = Misc(head_tasks, None)
            for task in head_tasks:
                pe_misc(pe, m, task, None)

            with pe.Fori(0, SEQS) as b:
                m = Misc(loop_tasks, b)
                pe.wait_ge(s_mA, m.taken("A"))
                pe.wait_ge(s_mD, m.taken("D"))
                for s in range(STEPS):
                    if s < NUB:
                        t, g = divmod(s, NU)
                        sp_ = S_ps[s % 2]
                        pe.wait_ge(s_shift, NUB * b + s + 1)
                        if g < H // G:
                            nc.tensor.matmul(sp_[:, :].rearrange("p (g k) -> p g k", g=G), identb[:, :],
                                             band[:, min(t, 1), :].unsqueeze(1).to_broadcast([P, G, P]),
                                             start=True, stop=False)
                            for n in range(G):
                                h = unit_head(g, n)
                                r = 32 * g
                                K_ = Kt[h % 2][r:r + 32, h // 8, :, :]
                                for q in range(2):
                                    keys = (K_[:, 2 * t:2 * t + 2, :][:, ::-1, :] if q == 0
                                            else K_[:, 2 * t + 1:2 * t + 3, :])
                                    mm = nc.tensor.matmul(
                                        sp_[W * q:W * (q + 1), n * P:(n + 1) * P].rearrange("p (a k) -> p a k", a=2),
                                        Qt[r:r + 32, h // 8, t * P + W * q:t * P + W * (q + 1)], keys,
                                        start=False, stop=n == G - 1)
                        else:
                            nc.tensor.matmul(sp_[:, :].rearrange("p (h n) -> p h n", h=LH), identb[:, :],
                                             latm[:, t, :].unsqueeze(1).to_broadcast([P, LH, NL]),
                                             start=True, stop=False)
                            mm = nc.tensor.matmul(sp_[:, :], Gt[:, t * P:(t + 1) * P],
                                                  bdK[:, :, :].rearrange("p h n -> p (h n)"), start=False, stop=True)
                        mm.then_inc(s_S, 1)
                    u = s - 1
                    if 0 <= u < NUB:
                        pe.wait_ge(s_exp, NUB * b + u + 1)
                        pe.wait_ge(s_pT, NUB * b + u + 1)
                        for n in range(G):
                            mm = nc.tensor.transpose(T_ps[u % 2][:, n * P:(n + 1) * P],
                                                     prob[:, u % 2, n * P:(n + 1) * P], c_ident)
                        mm.then_inc(s_T, 1)
                    u = s - 2
                    if 0 <= u < NUB:
                        t, g = divmod(u, NU)
                        if g == 0:
                            pe.wait_ge(s_O, TS * b + t + 1)
                        pe.wait_ge(s_pT, 2 + NUB * b + u + 1)
                        for n in range(G):
                            if g < H // G:
                                h = unit_head(g, n)
                                for q, vals in ((0, Ve), (1, Vo)):
                                    mm = nc.tensor.matmul(
                                        O_ps[t % 2][W * q:W * (q + 1), h * OW:(h + 1) * OW],
                                        probT[u % 2][:, n * P + W * q:n * P + W * (q + 1)],
                                        vals[:, t, h, :], start=True, stop=True)
                            else:
                                c = (H + 2 * n) * OW
                                mm = nc.tensor.matmul(O_ps[t % 2][:, c:c + 2 * OW], probT[u % 2][:, n * P:(n + 1) * P],
                                                      bdV[:, n, :, :].rearrange("p a d -> p (a d)"),
                                                      start=True, stop=True)
                        mm.then_inc(s_PV, 1)
                    for task in plan[s]:
                        pe_misc(pe, m, task, b)
            pe.wait_ge(s_mA, Misc(loop_tasks, SEQS).taken("A"))
            pe.wait_ge(s_mD, Misc(loop_tasks, SEQS).taken("D"))
            for part, k in ALL_PARTS:
                pe_choice(pe, 0, part, k)
            for q in range(GT):
                pe_rows(pe, 0, q)
            with pe.Fori(0, E - 1) as e:
                pe_expert(pe, e, False)
            pe_expert(pe, E - 1, True)

        CH = {"n": 0}

        def chain(dve, ins_, base=0):
            CH["n"] += 1
            ins_.then_inc(s_v, 1)
            dve.wait_ge(s_v, base + CH["n"])

        def dve_embed(dve, bb, base):
            par = bb & 1 if not isinstance(bb, int) else bb % 2

            def res(t):
                return hres[:, bass.ds(par, 1), t, :].rearrange("p a d -> p (a d)")

            def indices():
                nc.vector.tensor_copy(seg_now[:, :].unsqueeze(2), seg_all[:, :, bass.ds(bb, 1)])
                nc.vector.tensor_copy(idx_now[:, :].unsqueeze(2), idx_all[:, :, bass.ds(bb, 1)]).then_inc(s_idx, 1)
                dve.wait_ge(s_idx, bb + 1)

            def first(t):
                dve.wait_ge(s_rows[t], 16 * bb + 16)
                chain(dve, nc.vector.scalar_tensor_tensor(out=res(t), in0=rows[:, t, :], scalar=float(D) ** 0.5,
                                                          in1=P16[:, t, :], op0=ALU.mult, op1=ALU.add), base)
                nc.vector.scalar_tensor_tensor(out=res(t), in0=D16[:, :], scalar=seg_now[:, t:t + 1],
                                               in1=res(t), op0=ALU.mult, op1=ALU.add).then_inc(s_h0, 1)
                dve.wait_ge(s_h0, TS * bb + t + 1)
                stand(dve)
                chain(dve, nc.vector.bn_stats(st0[:, :], res(t)), base)
                stand(dve)
                chain(dve, nc.vector.bn_aggr(mv0[:, t, :], st0[:, :]), base)
                nc.vector.tensor_scalar(ve0[:, t:t + 1], mv0[:, t, 1:2], EPS, None, ALU.add).then_inc(s_var0, 1)

            def second(t, m):
                if t >= 2:
                    dve.wait_ge(s_misc, m.done(("ET", t - 2)))
                dve.wait_ge(s_rs0, TS * bb + t + 1)
                nc.vector.tensor_scalar(xn[:, t % 2, :], res(t), mv0[:, t, 0:1], rs0[:, t:t + 1],
                                        ALU.subtract, ALU.mult).then_inc(s_xn, 1)

            def pool_latents(m):
                dve.wait_ge(s_mA, m.out(("ET", TS - 1)))
                chain(dve, nc.vector.tensor_reduce(
                    xp[:, :, 0, :], x1T[:, :, :].rearrange("p c (n k) -> p c n k", n=NL), AX.X, ALU.add), base)
                nc.vector.tensor_copy(xp[:, :, 1, :], xp[:, :, 0, :]).then_inc(s_xp, 1)
            return indices, first, second, pool_latents

        def dve_misc(dve, m, task, b, base):
            name, t = task
            if TAKER[name] != "D":
                return
            bank = m.bank(task)
            dve.wait_ge(s_misc, m.done(task))
            if name == "K":
                for j in range(2):
                    ins_ = nc.vector.tensor_scalar(Kt[j][:, t, 1:, :].rearrange("p a k -> p (a k)"), bank[:, :],
                                                   c_parity[:, j:j + 1], None, ALU.mult)
                ins_.then_inc(s_mD, 1)
            elif name == "PK":
                nc.vector.tensor_tensor(bdK[:, :, :], bank[:, 0:NL].unsqueeze(1).to_broadcast([P, LH, NL]),
                                        c_own.unsqueeze(2).to_broadcast([P, LH, NL]), ALU.mult).then_inc(s_mD, 1)
            elif name == "PV":
                for r in range(2):
                    ins_ = nc.vector.tensor_scalar(
                        bdV[NL * r:NL * (r + 1), :, r, 0:HD],
                        bank[NL * r:NL * (r + 1), 0:LD].rearrange("p (a r d) -> p a r d", r=2, d=HD)[:, :, r, :],
                        float(NL) / S, None, ALU.mult)
                ins_.then_inc(s_mD, 1)
            elif name == "RO":
                nc.vector.tensor_tensor(r2[:, :, :], bank[:, 0:D].rearrange("p (h d) -> p h d", h=H),
                                        sg[:, H:2 * H].unsqueeze(2).to_broadcast([P, H, HD]), ALU.mult).then_inc(s_mD, 1)
                dve.wait_ge(s_mD, m.out(task))
                nc.vector.tensor_tensor(mix[:, :].rearrange("p (h d) -> p h d", h=H), loc[:, :, :], r2[:, :, :],
                                        ALU.add).then_inc(s_mix, 1)
            elif name == "WO":
                dve.wait_ge(s_h1out[t % 2], 16 * (TS // 2 * b + t // 2) + 16)
                nc.vector.tensor_tensor(h1[:, t % 2, :],
                                        hres[:, bass.ds(b & 1, 1), t, :].rearrange("p a d -> p (a d)"),
                                        bank[:, 0:D], ALU.add).then_inc(s_mD, 1)
                dve.wait_ge(s_mD, m.out(task))
                chain(dve, nc.vector.bn_stats(st1[:, :], h1[:, t % 2, :]), base)
                stand(dve)
                chain(dve, nc.vector.bn_aggr(mv1[:, :], st1[:, :]), base)
                nc.vector.tensor_scalar(ve1[:, :], mv1[:, 1:2], 1.0 + EPS, EPS * EPS, ALU.mult, ALU.add)\
                    .then_inc(s_var1, 1)
            elif name == "SC":
                nc.vector.tensor_tensor(score[:, :, bass.ds(TS * b + t, 1)], bank[:, 0:E].unsqueeze(2),
                                        kb[:, :].unsqueeze(2), ALU.add).then_inc(s_mD, 1)

        def dve_outputs(dve, b, t, m, base):
            O = O_ps[t % 2][:, 0:(H + LH) * OW].rearrange("p (h d) -> p h d", d=OW)
            dve.wait_ge(s_PV, NUB * b + NU * (t + 1))
            nc.vector.tensor_scalar(sg[:, :], gt[:, t, :], 0.5, 0.5, ALU.mult, ALU.add)
            chain(dve, nc.vector.reciprocal(rc[:, :].unsqueeze(2), O[:, :, HD:OW]), base)
            nc.vector.tensor_tensor(rem[:, :, :], O[:, H:, 0:HD],
                                    rc[:, H:].unsqueeze(2).to_broadcast([P, LH, HD]), ALU.mult).then_inc(s_rem, 1)
            chain(dve, nc.vector.tensor_tensor(cl[:, :], rc[:, 0:H], sg[:, 0:H], ALU.mult), base)
            nc.vector.tensor_tensor(loc[:, :, :], O[:, 0:H, 0:HD],
                                    cl[:, :].unsqueeze(2).to_broadcast([P, H, HD]), ALU.mult).then_inc(s_O, 1)

        def dve_as_float(dve, src, dst, width, base):
            chain(dve, nc.vector.tensor_scalar(flip[:, 0:width], src, 31, -1 << 31,
                                               ALU.arith_shift_right, ALU.bitwise_or), base)
            chain(dve, nc.vector.scalar_tensor_tensor(out=dst, in0=src, scalar=0x7FFFFFFF, in1=flip[:, 0:width],
                                                      op0=ALU.bitwise_xor, op1=ALU.bitwise_xor), base)

        def dve_choice(dve, n, part, k, base):
            if part == "radix":
                if k == 0:
                    chain(dve, nc.vector.scalar_tensor_tensor(
                        out=act_s[:, :].unsqueeze(1), in0=taken[:, :].unsqueeze(1), scalar=TAKEN,
                        in1=score[:, bass.ds(n, 1), :], op0=ALU.mult, op1=ALU.add), base)
                    chain(dve, nc.vector.memset(thr[:, :], 0), base)
                chain(dve, nc.vector.tensor_tensor(cand[:, :], digits[:, k, :],
                                                   thr[:, :].to_broadcast([P, RADIX - 1]), ALU.bitwise_or), base)
                dve_as_float(dve, cand[:, :], cval[:, :], RADIX - 1, base)
                for c in range(RADIX - 1):
                    ins_ = nc.vector.tensor_scalar(hits[:, :], act_s[:, :], cval[:, c:c + 1].bitcast(F32), None,
                                                   ALU.is_ge, ALU.add, accum_out=counts[:, c:c + 1])
                    if c < RADIX - 2:
                        chain(dve, ins_, base)
                ins_.then_inc(s_cand, 1)
                dve.wait_ge(s_total, DIGITS * n + k + 1)
                chain(dve, nc.vector.tensor_scalar(over[:, :], M_ps[0][:, 0:RADIX - 1], float(C), None,
                                                   ALU.is_ge, ALU.add, accum_out=nover[:, :]), base)
                chain(dve, nc.vector.tensor_scalar(delta[:, :], nover[:, :], float(2 ** (32 - BITS * (k + 1))), None,
                                                   ALU.mult), base)
                chain(dve, nc.vector.tensor_tensor(thr[:, :], thr[:, :], delta[:, :].bitcast(I32),
                                                   ALU.bitwise_or), base)
            elif part == "ties":
                dve_as_float(dve, thr[:, :], cval[:, 0:1], 1, base)
                T_ = cval[:, 0:1].bitcast(F32)
                chain(dve, nc.vector.tensor_scalar(above[:, :], act_s[:, :], T_, None, ALU.is_gt, ALU.add,
                                                   accum_out=nabove[:, :]), base)
                nc.vector.tensor_scalar(equal[:, :], act_s[:, :], T_, None, ALU.is_equal).then_inc(s_cut, 1)
                dve.wait_ge(s_ties, n + 1)
                chain(dve, nc.vector.tensor_scalar(need[:, :], M_ps[0][:, 2 * P:2 * P + 1], -1.0, float(C),
                                                   ALU.mult, ALU.add), base)
                dve_prefix(dve, base)
                chain(dve, nc.vector.scalar_tensor_tensor(out=chosen[:, :], in0=rank[:, :], scalar=need[:, :],
                                                          in1=equal[:, :], op0=ALU.is_lt, op1=ALU.mult), base)
                chain(dve, nc.vector.tensor_tensor(chosen[:, :], chosen[:, :], above[:, :], ALU.add), base)
                nc.vector.tensor_tensor(taken[:, :], taken[:, :], chosen[:, :], ALU.add)
                nc.vector.tensor_copy(chosenb[:, :], chosen[:, :]).then_inc(s_sel, 1)
                dve.wait_ge(s_sel, n + 1)
            elif part == "pos":
                dve.wait_ge(s_pos, n + 1)
                dve_prefix(dve, base)
                chain(dve, nc.vector.tensor_copy(ranki[:, :], rank[:, :]), base)
                chain(dve, nc.vector.tensor_scalar(rlowi[:, :], ranki[:, :], P - 1, None, ALU.bitwise_and), base)
                chain(dve, nc.vector.tensor_scalar(ranki[:, :], ranki[:, :], 7, None, ALU.arith_shift_right), base)
                chain(dve, nc.vector.tensor_copy(rhigh[:, :], ranki[:, :]), base)
                chain(dve, nc.vector.scalar_tensor_tensor(out=rlow[:, :], in0=rlowi[:, :], scalar=1.0,
                                                          in1=chosen[:, :], op0=ALU.add, op1=ALU.mult), base)
                chain(dve, nc.vector.tensor_scalar(rlow[:, :], rlow[:, :], -1.0, None, ALU.add), base)
                chain(dve, nc.vector.tensor_tensor(ohA[:, :, :], rhigh[:, :].unsqueeze(2).to_broadcast([P, NT, CT]),
                                                   laneb[:, 0:CT].unsqueeze(1).to_broadcast([P, NT, CT]),
                                                   ALU.is_equal), base)
                nc.vector.tensor_scalar(ohP[:, :, :], ohA[:, :, :], c_part, None, ALU.mult)
                nc.vector.scalar_tensor_tensor(out=ohT[:, :, :], in0=ohA[:, :, :], scalar=float(P),
                                               in1=laneb[:, 0:NT].unsqueeze(2).to_broadcast([P, NT, CT]),
                                               op0=ALU.mult, op1=ALU.mult).then_inc(s_ohA, 1)
            elif part == "list":
                if not (isinstance(n, int) and k < 2):
                    dve.wait_ge(s_used, LC * n + k - 1)
                for j in range(LT):
                    ins_ = nc.vector.tensor_scalar(ohB[:, k % 2, j, :], laneb[:, :],
                                                   rlow[:, k * LT + j:k * LT + j + 1], None, ALU.is_equal)
                ins_.then_inc(s_ohB, 1)
                if k == LC - 1:
                    dve.wait_ge(s_used, LC * n + LC)
                    nc.vector.tensor_copy(idx_next[:, :], LPS).then_inc(s_next, 1)

        def dve_prefix(dve, base):
            totals = M_ps[0][:, P:P + NT]
            chain(dve, nc.vector.tensor_copy(rank[:, :], totals), base)
            chain(dve, nc.vector.tensor_tensor_scan(cum[:, :], rank[:, :], zeros[:, :], 0.0, ALU.add, ALU.add), base)
            chain(dve, nc.vector.tensor_tensor(cum[:, :], cum[:, :], rank[:, :], ALU.subtract), base)
            chain(dve, nc.vector.tensor_tensor(rank[:, :], cum[:, :], M_ps[0][:, 0:NT], ALU.add), base)

        def dve_stats(dve, gi, half, base):
            for q in range(GT):
                dve.wait_ge(s_gr[q], 16 * gi + 16)
                nc.vector.bn_stats(st2[:, q, :], hrow[:, half, q, :])
            chain(dve, nc.vector.memset(r1[:, :], 1.0), base)
            stand(dve)
            for q in range(GT):
                ins_ = nc.vector.bn_aggr(mv2[:, q, :], st2[:, q, :])
            chain(dve, ins_, base)
            nc.vector.tensor_scalar(ve2[:, 0, :].unsqueeze(2), mv2[:, :, 1:2], 1.0 + EPS, EPS * EPS, ALU.mult, ALU.add)
            nc.vector.tensor_scalar(ve2[:, 1, :].unsqueeze(2), mv2[:, :, 1:2], EPS, None, ALU.add).then_inc(s_var2, 1)
            dve.wait_ge(s_rs2, gi + 1)
            nc.vector.tensor_scalar(r1[:, :], rs2[:, 1, :], 1.0, None, ALU.add)
            chain(dve, nc.vector.scalar_tensor_tensor(out=nmr[:, :].unsqueeze(2), in0=mv2[:, :, 0:1], scalar=-1.0,
                                                      in1=rs2[:, 1, :].unsqueeze(2), op0=ALU.mult, op1=ALU.mult), base)

        def dve_rows(dve, gi, q, half):
            if q >= 2:
                dve.wait_ge(s_yT, GT * gi + q - 1)
            nc.vector.tensor_scalar(y2[:, q % 2, :], hrow[:, half, q, :], mv2[:, q, 0:1], rs2[:, 0, q:q + 1],
                                    ALU.subtract, ALU.mult).then_inc(s_y2, 1)
            nc.vector.tensor_scalar(hrow[:, half, q, :], hrow[:, half, q, :], r1[:, q:q + 1], nmr[:, q:q + 1],
                                    ALU.mult, ALU.add)

        def dve_expert(dve, e, last, base):
            dve.wait_ge(s_free, 2 + CT * e)
            nc.vector.tensor_copy(idx_cur[:, :], idx_next[:, :]).then_inc(s_cur, 1)
            dve.wait_ge(s_hid, 2 + FC * GR * e)
            nc.vector.tensor_copy(b1[:, :].unsqueeze(1), b1_all[:, bass.ds(e, 1), :]).then_inc(s_b1, 1)
            for g in range(GR):
                gi = GR * e + g
                more = g + 1 < GR or not last
                for m in range(FC):
                    if not last:
                        for part, k in CHOICE.get((g, m), []):
                            dve_choice(dve, e + 1, part, k, base)
                    if m == STATS_AT and more:
                        dve_stats(dve, gi + 1, (g + 1) % 2 if g + 1 < GR else 0, base)
                        dve_rows(dve, gi + 1, 0, (g + 1) % 2 if g + 1 < GR else 0)
                for q in range(GT):
                    if q + 1 < GT and more:
                        dve_rows(dve, gi + 1, q + 1, (g + 1) % 2 if g + 1 < GR else 0)
                    dve.wait_ge(s_l2, GT * gi + q + 1)
                    dve.wait_ge(s_free, GT * gi + q + 1)
                    nc.vector.tensor_tensor(orow[:, q % 2, :], O_ps[q % 2][:, 0:D], hrow[:, g % 2, q, :],
                                            ALU.add).then_inc(s_fin, 1)
                    if not last:
                        for part, k in CHOICE.get((g, FC + q), []):
                            dve_choice(dve, e + 1, part, k, base)

        @block.vector
        def _(dve):
            dve.wait_ge(s_load, 16 * LOADS)
            chain(dve, nc.vector.tensor_copy(xf[:, :], xi[:, :]))
            chain(dve, nc.vector.tensor_scalar(xw[:, :], xf[:, :], 0.0, float(V), ALU.is_lt, ALU.mult))
            chain(dve, nc.vector.tensor_tensor(xw[:, :], xw[:, :], xf[:, :], ALU.add))
            chain(dve, nc.vector.tensor_scalar(xw[:, :], xw[:, :], 0.0, float(V - 1), ALU.max, ALU.min))
            chain(dve, nc.vector.tensor_scalar(xf[:, :], xf[:, :], float(SEP), None, ALU.is_equal))
            nc.vector.tensor_tensor_scan(xs[:, :], xf[:, :], xf[:, :], 0.0, ALU.max, ALU.max).then_inc(s_init, 1)
            nc.vector.tensor_copy(identb[:, :], c_ident)
            nc.vector.tensor_copy(beforeb[:, :], c_before)
            nc.vector.tensor_copy(laneb[:, :], c_lane)
            nc.vector.memset(onesb[:, :], 1.0)
            nc.vector.memset(taken[:, :], 0.0)
            nc.vector.memset(zeros[:, :], 0.0)
            nc.vector.tensor_copy(band[:, :, :].rearrange("p a k -> p (a k)"), c_band)
            nc.vector.tensor_copy(latm[:, :, :].rearrange("p a k -> p (a k)"), c_lat)
            nc.vector.memset(Kt[0][:, :, 0, :], 0.0)
            nc.vector.memset(Kt[1][:, :, 0, :], 0.0)
            nc.vector.memset(Vo[:, :, :, HD:OW], 1.0)
            chain(dve, nc.vector.memset(Ve[:, :, :, :], 0.0))
            nc.vector.memset(Ve[:, :, :, HD:OW], 1.0)
            chain(dve, nc.vector.memset(bdV[:, :, :, :], 0.0))
            nc.vector.memset(bdV[0:NL, :, 0, HD:OW], 1.0)
            nc.vector.memset(bdV[NL:P, :, 1, HD:OW], 1.0)
            chain(dve, nc.vector.tensor_tensor(P16[:, :, :], P16[:, :, :],
                                               segs[:, 0:1, :].to_broadcast([P, TS, D]), ALU.add))
            chain(dve, nc.vector.tensor_tensor(D16[:, :], segs[:, 1, :], segs[:, 0, :], ALU.subtract))
            chain(dve, nc.vector.tensor_scalar(P16[:, :, :], P16[:, :, :], float(D) ** 0.5, None, ALU.mult))
            chain(dve, nc.vector.tensor_scalar(D16[:, :], D16[:, :], float(D) ** 0.5, None, ALU.mult))
            for j in range(2):
                chain(dve, nc.vector.tensor_tensor(gprod[:, :, j, :], wq[:, :, :],
                                                   gates[:, j:j + 1, :].to_broadcast([P, KC, D]), ALU.mult))
                nc.vector.tensor_reduce(wvg[:, :, D + H * j:D + H * (j + 1)],
                                        gprod[:, :, j, :].rearrange("p c (h d) -> p c h d", h=H), AX.X, ALU.add)
            nc.vector.memset(mx[:, :, :], 0.0).then_inc(s_init, 2)
            dve.wait_ge(s_setT, 1)
            nc.vector.tensor_copy(idx_all[:, :, 0:SEQS], M_ps[0][:, 0:TS * SEQS].rearrange("p (t b) -> p t b", t=TS))
            nc.vector.tensor_copy(idx_all[:, :, SEQS:SEQS + 1],
                                  M_ps[0][:, 0:TS * SEQS].rearrange("p (t b) -> p t b", t=TS)[:, :, 0:1])
            nc.vector.tensor_copy(seg_all[:, :, 0:SEQS],
                                  M_ps[0][:, TS * SEQS:2 * TS * SEQS].rearrange("p (t b) -> p t b", t=TS))
            nc.vector.tensor_copy(seg_all[:, :, SEQS:SEQS + 1],
                                  M_ps[0][:, TS * SEQS:2 * TS * SEQS].rearrange("p (t b) -> p t b", t=TS)[:, :, 0:1])
            for c in range(KC):
                nc.vector.tensor_copy(lnb_row[:, c, :], M_ps[1][:, 32 + KC + c:33 + KC + c].to_broadcast([P, P]))
            nc.vector.tensor_copy(ln[:, :], M_ps[1][:, 32:32 + 2 * KC])
            nc.vector.tensor_copy(b1_all[:, :, :], M_ps[1][:, 128:128 + E * FC].rearrange("p (e m) -> p e m", e=E))
            nc.vector.tensor_copy(cenT[:, :, :], M_ps[1][:, 0:KC * E].rearrange("p (c e) -> p c e", c=KC))\
                .then_inc(s_setE, 2)
            dve.wait_ge(s_setT, 2)
            nc.vector.tensor_copy(kb[:, :], M_ps[1][:, 64:64 + E])
            nc.vector.tensor_tensor(cenT[:, :, :], cenT[:, :, :],
                                    ln[:, 0:KC].unsqueeze(2).to_broadcast([P, KC, E]), ALU.mult).then_inc(s_setE, 2)
            dve.wait_ge(s_setE, 4)
            nc.vector.memset(mx[:, :, :], 0.0).then_inc(s_shift, 2)
            nc.vector.memset(st0[:, :], 0.0).then_inc(s_O, 2)
            nc.vector.memset(st1[:, :], 0.0).then_inc(s_h1out[0], 16)
            nc.vector.memset(mv1[:, :], 0.0).then_inc(s_h1out[1], 16)

            m = Misc(head_tasks, None)
            indices, first, second, pool_latents = dve_embed(dve, 0, 0)
            indices()
            for t in range(TS):
                first(t)
            for t in range(TS):
                second(t, m)
            pool_latents(m)
            for task in head_tasks:
                dve_misc(dve, m, task, None, 0)

            head_chain = CH["n"]
            CH["n"] = 0
            PER = NUB + 7 * TS + 1
            with dve.Fori(0, SEQS) as b:
                base = PER * b + head_chain
                m = Misc(loop_tasks, b)
                indices, first, second, pool_latents = dve_embed(dve, b + 1, base)
                indices()
                for s in range(STEPS):
                    if s < NUB:
                        t, g = divmod(s, NU)
                        heads = G if g < H // G else LH
                        sc = S_ps[s % 2][:, :].rearrange("p (h k) -> p h k", h=heads)
                        top = mx[:, s % 2, 0:heads]
                        dve.wait_ge(s_S, NUB * b + s + 1)
                        chain(dve, nc.vector.tensor_reduce(top, sc, AX.X, ALU.max), base)
                        nc.vector.tensor_tensor(prob[:, s % 2, :].rearrange("p (h k) -> p h k", h=heads), sc,
                                                top.unsqueeze(2).to_broadcast([P, heads, 512 // heads]),
                                                ALU.subtract).then_inc(s_shift, 1)
                    for t in range(TS):
                        if s == NU * t:
                            first(t)
                        if s == NU * t + 2:
                            second(t, m)
                        if s == NU * (t + 1) + 1:
                            dve_outputs(dve, b, t, m, base)
                        if s == NU * t + 12:
                            dve.wait_ge(s_rs1, TS * b + t + 1)
                            nc.vector.tensor_scalar(y[:, :], h1[:, t % 2, :], mv1[:, 0:1], rs1[:, :],
                                                    ALU.subtract, ALU.mult).then_inc(s_y, 1)
                    if s == NUB - 1:
                        pool_latents(m)
                    for task in plan[s]:
                        dve_misc(dve, m, task, b, base)
            assert CH["n"] == PER, CH["n"]

            CH["n"] = 0
            base = PER * SEQS + head_chain
            dve.wait_ge(s_mD, Misc(loop_tasks, SEQS).taken("D"))
            nc.vector.memset(mx[:, :, :], 0.0).then_inc(s_fin, GT)
            nc.vector.memset(st0[:, :], 0.0).then_inc(s_free, 2)
            for part, k in ALL_PARTS:
                dve_choice(dve, 0, part, k, base)
            dve_stats(dve, 0, 0, base)
            for q in range(GT):
                dve_rows(dve, 0, q, 0)
            base += CH["n"]
            CH["n"] = 0
            PER2 = 8 * DIGITS + 3 * GR + 23
            with dve.Fori(0, E - 1) as e:
                dve_expert(dve, e, False, PER2 * e + base)
            assert CH["n"] == PER2, CH["n"]
            base += PER2 * (E - 1)
            CH["n"] = 0
            dve_expert(dve, E - 1, True, base)


NAMES = {"x": "x", "tok_table": "L0_tok_tok_table", "pos_table": "L0_tok_pos_table", "seg_table": "L0_tok_seg_table",
         "wq": "L0_attn_wq", "wk": "L0_attn_wk", "wv": "L0_attn_wv", "wgq": "L0_attn_wgq", "wgk": "L0_attn_wgk",
         "wgv": "L0_attn_wgv", "r_out_w": "L0_attn_r_out_w", "gate_local_w": "L0_attn_gate_local_w",
         "gate_remote_w": "L0_attn_gate_remote_w", "w_out": "L0_attn_w_out", "centroids": "L0_ffn_centroids",
         "ln_g": "L0_ffn_ln_g", "ln_b": "L0_ffn_ln_b", "w1": "L0_ffn_w1", "b1": "L0_ffn_b1", "w2": "L0_ffn_w2",
         "b2": "L0_ffn_b2"}


def kernel(**inputs):
    import concourse.bacc as bacc
    from concourse.bass_utils import run_bass_kernel_spmd

    given = {short: np.ascontiguousarray(inputs[name]) for short, name in NAMES.items()}
    seqs, S = given["x"].shape
    E, _, F = given["w1"].shape
    given["tables"], widths, given["digit_table"] = constants(S)

    nc = bacc.Bacc("TRN2", target_bir_lowering=False, num_devices=1)
    arrays, aps = {}, {}
    for name, a in given.items():
        arrays[f"in_{name}"] = a
        aps[name] = nc.dram_tensor(f"in_{name}", a.shape, mybir.dt.from_np(a.dtype), kind="ExternalInput").ap()
    out = nc.dram_tensor("out_rows", [seqs * S, D], F32, kind="ExternalOutput").ap()
    tower(nc, aps, out, aps["tables"], aps["digit_table"], widths, seqs, S, given["tok_table"].shape[0], F, E)
    r = run_bass_kernel_spmd(nc, [arrays], core_ids=[0])
    return np.asarray(r.results[0]["out_rows"]).reshape(seqs, S, D)
```

```python
from contextlib import ExitStack

import numpy as np

import concourse.bass as bass
from concourse import mybir
from concourse.alu_op_type import AluOpType as ALU

F32 = mybir.dt.float32
BF16 = mybir.dt.bfloat16
I32 = mybir.dt.int32
U32 = mybir.dt.uint32
ACT = mybir.ActivationFunctionType
AX = mybir.AxisListType

P = 128
D = 256
KC = D // P
H = 16
HD = D // H
LH = 8
LD = LH * HD
NL = 64
W = 64
SEP = 102
EPS = 1e-5
NEG = -1e30
G = 4
NU = H // G + 1
BITS = 4
RADIX = 1 << BITS
DIGITS = 32 // BITS
TAKEN = -3e38
GT = 4
RING = 4
T_LAG = 2
O_LAG = 3
OW = HD + 1


def unit_head(g, n):
    return 2 * g + n % 2 + H // 2 * (n // 2)


def constants(S):
    i = np.arange(P)
    ident = np.eye(P, dtype=np.float32)
    ring = (i[:, None] - i[None, :]) % P < W
    first = ring & ~((i[:, None] < W) & (i[None, :] >= W))
    band = np.stack([np.where(m, 0.0, NEG) for m in (first, ring)], 1)
    tiles = S // P
    tok = np.arange(tiles)[None, :, None] * P + i[:, None, None]
    lat = np.where(np.arange(NL)[None, None, :] <= tok // (S // NL), 0.0, NEG)
    parity = np.stack([(i // HD) % 2 == 0, (i // HD) % 2 == 1], 1)
    own = (i[:, None] // HD == np.arange(LH)[None, :]) * (NL / S)
    before = i[:, None] < i[None, :]
    lane = np.broadcast_to(i[None, :], (P, P))
    f = lambda a: np.ascontiguousarray(a.reshape(P, -1).astype(np.float32))
    cols = [f(ident), f(band), f(lat), f(parity), f(own), f(before), f(lane), f(i)]
    digit = np.arange(1, RADIX, dtype=np.int64)[None, :] << (32 - BITS * (1 + np.arange(DIGITS, dtype=np.int64)))[:, None]
    digits = np.broadcast_to(digit.astype(np.uint32).view(np.int32).reshape(1, -1), (P, DIGITS * (RADIX - 1)))
    return np.concatenate(cols, 1), [c.shape[1] for c in cols], np.ascontiguousarray(digits)


def tower(nc, ins, out, cin, din, widths, SEQS, S, V, F, E):
    TS = S // P
    TOK = SEQS * S
    NT = TOK // P
    NUB = TS * NU
    C = TOK // E
    CT = C // P
    GR = CT // GT
    FC = F // P
    LC = min(8, NT // 8)
    LT = NT // LC
    assert S // NL * NL == S and TS == 4 and NT <= P and CT == GR * GT

    ctx = ExitStack()
    with ctx:
        attention = ExitStack()

        def sb(name, shape, dt=F32, stack=ctx):
            return stack.enter_context(nc.sbuf_tensor(name, shape, dt))

        def sba(name, shape, dt=F32):
            return sb(name, shape, dt, attention)

        def sem(name):
            return ctx.enter_context(nc.semaphore(name))

        h1_rows = nc.dram_tensor("h1_rows", [TOK, D], F32, kind="Internal").ap()
        h1_tiles = h1_rows.rearrange("(n p) d -> p n d", p=P)

        S_ps = [ctx.enter_context(nc.psum_tensor(f"S_ps{j}", [P, 512], F32)) for j in range(2)]
        T_ps = [ctx.enter_context(nc.psum_tensor(f"T_ps{j}", [P, 512], F32)) for j in range(2)]
        O_ps = [ctx.enter_context(nc.psum_tensor(f"O_ps{j}", [P, 512], F32)) for j in range(2)]
        M_ps = [ctx.enter_context(nc.psum_tensor(f"M_ps{j}", [P, 512], F32)) for j in range(2)]

        cst = sb("cst", [P, sum(widths)])
        at = np.cumsum([0] + widths)
        c_ident, c_band, c_lat, c_parity, c_own, c_before, c_lane, c_part = (
            cst[:, int(at[n]):int(at[n + 1])] for n in range(len(widths)))
        identb = sb("identb", [P, P], BF16)
        band = sb("band", [P, 2, P], BF16)
        latm = sb("latm", [P, TS, NL], BF16)
        cen = sb("cen", [E, D])
        cenT = sb("cenT", [P, KC, E])
        ln_rows = sb("ln_rows", [2 * KC, P])
        ln = sb("ln", [P, 2 * KC])
        lnb_row = sb("lnb_row", [P, KC, P])
        kb = sb("kb", [P, E])
        idx_all = sb("idx_all", [P, TS, SEQS + 2], I32)
        seg_all = sb("seg_all", [P, TS, SEQS + 2])
        idx_now = sb("idx_now", [P, TS], I32)
        seg_now = sb("seg_now", [P, TS])
        mhalf = sb("mhalf", [P, 1])
        mx = sb("mx", [P, 2, LH])
        rc = sb("rc", [P, H + LH])
        sg = sb("sg", [P, 2 * H])
        cl = sb("cl", [P, H])
        h1 = sb("h1", [P, 2, D])
        st1 = sb("st1", [P, 6])
        mv1 = sb("mv1", [P, 2])
        ve1 = sb("ve1", [P, 1])
        rs1 = sb("rs1", [P, 1])
        y = sb("y", [P, D])
        yT = sb("yT", [P, KC, P])
        score = sb("score", [P, E, NT])

        digits = sb("digits", [P, DIGITS, RADIX - 1], I32)
        onesb = sb("onesb", [P, P], BF16)
        beforeb = sb("beforeb", [P, P], BF16)
        laneb = sb("laneb", [P, P], BF16)
        taken = sb("taken", [P, NT])
        zeros = sb("zeros", [P, NT])
        act_s = sb("act_s", [P, NT])
        thr = sb("thr", [P, 1], I32)
        cand = sb("cand", [P, RADIX - 1], I32)
        flip = sb("flip", [P, RADIX - 1], I32)
        cval = sb("cval", [P, RADIX - 1], I32)
        counts = sb("counts", [P, RADIX - 1], BF16)
        over = sb("over", [P, RADIX - 1])
        nover = sb("nover", [P, 1])
        delta = sb("delta", [P, 1], U32)
        above = sb("above", [P, NT])
        equal = sb("equal", [P, NT], BF16)
        nabove = sb("nabove", [P, 1], BF16)
        need = sb("need", [P, 1])
        cum = sb("cum", [P, NT])
        rank = sb("rank", [P, NT])
        chosen = sb("chosen", [P, NT])
        chosenb = sb("chosenb", [P, NT], BF16)
        ranki = sb("ranki", [P, NT], I32)
        rlowi = sb("rlowi", [P, NT], I32)
        rlow = sb("rlow", [P, NT])
        rhigh = sb("rhigh", [P, NT], BF16)
        idx_next = sb("idx_next", [P, CT], I32)
        idx_cur = sb("idx_cur", [P, CT], I32)
        b1_rows = sb("b1_rows", [E * FC, P])
        b1_all = sb("b1_all", [P, E, FC])
        st2 = sb("st2", [P, GT, 6])
        mv2 = sb("mv2", [P, GT, 2])
        ve2 = sb("ve2", [P, 2, GT])
        rs2 = sb("rs2", [P, 2, GT])
        r1 = sb("r1", [P, GT])
        nmr = sb("nmr", [P, 2, GT])
        wq = sba("wq", [P, KC, D])
        wk = sba("wk", [P, KC, D])
        wvg = sba("wvg", [P, KC, D + 2 * H])
        wgq = sba("wgq", [P, KC, LD])
        wgk = sba("wgk", [P, KC, LD])
        wgv = sba("wgv", [P, KC, LD])
        wro = sba("wro", [P, D])
        wout = sba("wout", [P, KC, D])
        gates = sba("gates", [P, 2, D])
        gprod = sba("gprod", [P, KC, 2, D])
        segs = sba("segs", [P, 2, D])
        P16 = sba("P16", [P, TS, D])
        D16 = sba("D16", [P, D])
        xi = sba("xi", [SEQS, S], I32)
        xf = sba("xf", [SEQS, S])
        xw = sba("xw", [SEQS, S])
        xs = sba("xs", [SEQS, S])
        rows = sba("rows", [P, TS, D])
        hres = sba("hres", [P, 2, TS, D])
        st0 = sba("st0", [P, 6])
        mv0 = sba("mv0", [P, TS, 2])
        ve0 = sba("ve0", [P, TS])
        rs0 = sba("rs0", [P, TS])
        xn = sba("xn", [P, 2, D])
        x1T = sba("x1T", [P, KC, S])
        Qt = [sba(f"Qt{j}", [P, 2, S]) for j in range(2)]
        Kt = [sba(f"Kt{j}", [P, 2, 1 + S // W, 2, W]) for j in range(2)]
        Gt = [sba(f"Gt{j}", [P, S]) for j in range(2)]
        Vo = [sba(f"Vo{j}", [P, TS, H, OW]) for j in range(2)]
        Ve = [sba(f"Ve{j}", [P, TS + 1, H, OW]) for j in range(2)]
        gt = [sba(f"gt{j}", [P, TS, 2 * H]) for j in range(2)]
        xp = sba("xp", [P, KC, 2, NL])
        bdK = [sba(f"bdK{j}", [P, LH, NL]) for j in range(2)]
        bdV = [sba(f"bdV{j}", [P, LH // 2, 2, OW]) for j in range(2)]
        prob = sba("prob", [P, RING, 512])
        probT = [sba(f"probT{j}", [P, 512]) for j in range(2)]
        rem = sba("rem", [P, LH, HD])
        loc = sba("loc", [P, H, HD])
        remT = sba("remT", [P, P])
        r2 = sba("r2", [P, H, HD])
        mix = sba("mix", [P, D])
        mixT = sba("mixT", [P, KC, P])
        attention.close()
        hits = sb("hits", [P, RADIX - 1, NT], BF16)
        ohA = sb("ohA", [P, NT, CT], BF16)
        ohP = sb("ohP", [P, NT, CT], BF16)
        ohT = sb("ohT", [P, NT, CT], BF16)
        ohB = sb("ohB", [P, 2, LT, P], BF16)
        w1 = sb("w1", [P, KC, F])
        w2 = sb("w2", [P, FC, D])
        b1 = sb("b1", [P, FC])
        b2 = sb("b2", [P, D])
        hrow = sb("hrow", [P, 2, GT, D])
        y2 = sb("y2", [P, 2, D])
        hT = [sb(f"hT{j}", [P, KC, GT * P]) for j in range(2)]
        hid = sb("hid", [P, FC, GT * P])
        orow = sb("orow", [P, 2, D])

        s_load = sem("s_load")
        s_cand = sem("s_cand")
        s_total = sem("s_total")
        s_cut = sem("s_cut")
        s_ties = sem("s_ties")
        s_sel = sem("s_sel")
        s_pos = sem("s_pos")
        s_ohA = sem("s_ohA")
        s_ohB = sem("s_ohB")
        s_used = sem("s_used")
        s_next = sem("s_next")
        s_cur = sem("s_cur")
        s_gr = [sem(f"s_gr{q}") for q in range(GT)]
        s_var2 = sem("s_var2")
        s_rs2 = sem("s_rs2")
        s_scales = sem("s_scales")
        s_scaled = sem("s_scaled")
        s_y2 = sem("s_y2")
        s_yT = sem("s_yT")
        s_hT = sem("s_hT")
        s_l1 = sem("s_l1")
        s_hid = sem("s_hid")
        s_l2 = sem("s_l2")
        s_fin = sem("s_fin")
        s_add = sem("s_add")
        s_out = [sem(f"s_out{j}") for j in range(2)]
        s_free = sem("s_free")
        s_stand = sem("s_stand")
        s_w1 = sem("s_w1")
        s_w2 = sem("s_w2")
        s_b1 = sem("s_b1")
        s_b2 = sem("s_b2")
        s_init = sem("s_init")
        s_mh = sem("s_mh")
        s_setT = sem("s_setT")
        s_setE = sem("s_setE")
        s_idx = sem("s_idx")
        s_rows = [sem(f"s_rows{t}") for t in range(TS)]
        s_h0 = sem("s_h0")
        s_var0 = sem("s_var0")
        s_rs0 = sem("s_rs0")
        s_xn = sem("s_xn")
        s_xp = sem("s_xp")
        s_misc = sem("s_misc")
        s_mA = sem("s_mA")
        s_mD = sem("s_mD")
        s_S = sem("s_S")
        s_shift = sem("s_shift")
        s_exp = sem("s_exp")
        s_T = sem("s_T")
        s_pT = sem("s_pT")
        s_PV = sem("s_PV")
        s_O = sem("s_O")
        s_rem = sem("s_rem")
        s_mix = sem("s_mix")
        s_h1out = [sem(f"s_h1out{j}") for j in range(2)]
        s_var1 = sem("s_var1")
        s_rs1 = sem("s_rs1")
        s_y = sem("s_y")
        s_v = sem("s_v")

        def stand(eng):
            eng.sem_inc(s_stand, 1)

        TAKER = {"ET": "A", "RT": "A", "RO": "D", "MT": "A", "WO": "D", "YT": "A", "SC": "D",
                 "Q": "A", "K": "A", "G": "A", "PK": "D", "PV": "D", "V": "A"}
        TAIL = (("RT", 9), ("RO", 10), ("MT", 11), ("WO", 12), ("YT", 14), ("SC", 15))
        OUT_AT, Y_AT = 8, 13
        EMBED_AT, STAT_AT, NORM_AT, ET_AT = [0, 1, 4, 9], [1, 4, 5, 9], [2, 5, 6, 10], [3, 6, 7, 11]
        POOL_AT, IDX_AT = 12, 10
        LAG = {}
        plan = [[] for _ in range(NUB)]
        for t in reversed(range(TS)):
            for name, off in TAIL:
                step = NU * t + off
                LAG[name, t] = step // NUB
                plan[step % NUB].append((name, t))
        for t in range(TS):
            plan[ET_AT[t]].append(("ET", t))
        proj = {12: [("Q", 0)], 13: [("Q", 1), ("K", 0)], 14: [("K", 1)], 15: [("G", 0)], 16: [("PK", 0), ("V", 0)],
                17: [("V", 1), ("PV", 0)], 18: [("V", 2), ("V", 3)]}
        for step, tasks in proj.items():
            plan[step][:0] = tasks
        loop_tasks = [x for step in plan for x in step]
        lag = lambda x: LAG.get(x, 0)
        first_tasks = [x for x in loop_tasks if lag(x) == 0]
        last_tasks = [x for x in loop_tasks if lag(x) == 1]
        head_tasks = [("ET", t) for t in range(TS)] + [x for tasks in proj.values() for x in tasks]

        class Misc:

            def __init__(self, step, par=0):
                mine = lambda ts, e: sum(TAKER[x[0]] == e for x in ts)
                if isinstance(step, str):
                    self.tasks, self.prev, known, more = head_tasks, [], [], 0
                elif isinstance(step, int) and step == 0:
                    self.tasks, self.prev, known, more = first_tasks, head_tasks, head_tasks, 0
                else:
                    last = isinstance(step, int) and step == SEQS
                    self.tasks = last_tasks if last else loop_tasks
                    self.prev = first_tasks if isinstance(step, int) and step == 1 else loop_tasks
                    known, more = head_tasks + first_tasks, step - 1
                self.old = not (isinstance(step, str) or isinstance(step, int) and step == 0)
                self.new = self.tasks is not last_tasks
                self.n0 = more * len(loop_tasks) + len(known)
                self.parity = (len(known) + (par + 1) * len(loop_tasks) * self.old) % 2
                self.before = {e: more * mine(loop_tasks, e) + mine(known, e) for e in "AD"}

            def here(self, task):
                return task in self.tasks

            def bank(self, task):
                return M_ps[(self.parity + self.tasks.index(task)) % 2]

            def done(self, task):
                if task in self.tasks:
                    return self.n0 + (self.tasks.index(task) + 1)
                return self.n0 - (len(self.prev) - self.prev.index(task) - 1)

            def free(self, eng, task):
                k = self.tasks.index(task) - 2
                if k >= 0:
                    e, count = TAKER[self.tasks[k][0]], self.out(self.tasks[k])
                elif self.prev:
                    e = TAKER[self.prev[k][0]]
                    count = self.before[e] - sum(TAKER[x[0]] == e for x in self.prev[len(self.prev) + k + 1:])
                else:
                    return
                eng.wait_ge(s_mA if e == "A" else s_mD, count)

            def out(self, task, reader=None):
                e = TAKER[task[0]]
                if task in self.tasks and (reader is None or lag(reader) == lag(task)):
                    k = self.tasks.index(task)
                    return self.before[e] + sum(TAKER[x[0]] == e for x in self.tasks[:k + 1])
                return self.out_before(task)

            def out_before(self, task):
                e = TAKER[task[0]]
                k = self.prev.index(task)
                return self.before[e] - sum(TAKER[x[0]] == e for x in self.prev[k + 1:])

            def end(self, e):
                return self.before[e] + sum(TAKER[x[0]] == e for x in self.tasks)

        def units(s, m):
            def at(lag):
                u = s - lag
                if u >= 0:
                    return (0, u) if m.new else None
                return (1, u + NUB) if m.old else None
            return at

        LOADS = 20
        block = ctx.enter_context(nc.Block())

        @block.sync
        def _(sp):
            v1 = lambda a: a.rearrange("(c p) -> c p", p=P)
            v2 = lambda a: a.rearrange("(c p) n -> p c n", p=P)
            loads = [
                (xi[:, :], ins["x"]), (cst[:, :], cin), (digits[:, :, :].rearrange("p a b -> p (a b)"), din),
                (b1_rows[:, :], ins["b1"].rearrange("e (m p) -> (e m) p", p=P)),
                (segs[:, 0, :], ins["seg_table"][0:1, :].to_broadcast([P, D])),
                (segs[:, 1, :], ins["seg_table"][1:2, :].to_broadcast([P, D])),
                (P16[:, :, :], ins["pos_table"].rearrange("(t p) d -> p t d", p=P)),
                (wq[:, :, :], v2(ins["wq"])), (wk[:, :, :], v2(ins["wk"])),
                (wvg[:, :, 0:D], v2(ins["wv"])), (wgq[:, :, :], v2(ins["wgq"])),
                (wgk[:, :, :], v2(ins["wgk"])), (wgv[:, :, :], v2(ins["wgv"])),
                (wro[:, :], ins["r_out_w"]), (wout[:, :, :], v2(ins["w_out"])),
                (gates[:, 0, :], ins["gate_local_w"].rearrange("(a h) d -> a (h d)", a=1).to_broadcast([P, D])),
                (gates[:, 1, :], ins["gate_remote_w"].rearrange("(a h) d -> a (h d)", a=1).to_broadcast([P, D])),
                (cen[:, :], ins["centroids"]),
                (ln_rows[0:KC, :], v1(ins["ln_g"])), (ln_rows[KC:2 * KC, :], v1(ins["ln_b"])),
            ]
            for dst, src in loads:
                sp.dma_start(dst, src).then_inc(s_load, 16)
            assert len(loads) == LOADS

            def store(b, par):
                m = Misc(b, par)
                for task in m.tasks:
                    name, t = task
                    if name == "WO":
                        sp.wait_ge(s_mD, m.out(task))
                        sp.dma_start(h1_tiles[:, bass.ds(TS * (b - lag(task)) + t, 1), :],
                                     h1[:, t % 2, :].unsqueeze(1)).then_inc(s_h1out[t % 2], 16)

            store(0, 0)
            store(1, 1)
            with sp.Fori(1, SEQS // 2) as i:
                store(2 * i, 0)
                store(2 * i + 1, 1)
            store(SEQS, 0)
            sp.wait_ge(s_h1out[0], 16 * (NT // 2 + 1))
            sp.wait_ge(s_h1out[1], 16 * (NT // 2 + 1))
            for t in range(TS):
                sp.wait_ge(s_rows[t], 16 * (SEQS + 2))
            w1_v = ins["w1"].rearrange("e (c p) f -> p e c f", p=P)
            w2_v = ins["w2"].rearrange("e (m p) d -> p e m d", p=P)
            sp.dma_start(w1[:, :, :], w1_v[:, 0, :, :]).then_inc(s_w1, 16)
            sp.dma_start(w2[:, :, :], w2_v[:, 0, :, :]).then_inc(s_w2, 16)
            sp.dma_start(b2[:, :], ins["b2"][0:1, :].to_broadcast([P, D])).then_inc(s_b2, 16)
            with sp.Fori(0, E - 1) as e:
                src1 = w1_v[:, bass.ds(e + 1, 1), :, :].rearrange("p a c f -> p (a c) f")
                src2 = w2_v[:, bass.ds(e + 1, 1), :, :].rearrange("p a m d -> p (a m) d")
                srcb = ins["b2"][bass.ds(e + 1, 1), :].to_broadcast([P, D])
                sp.wait_ge(s_l1, FC * GR * e + FC * GR)
                sp.dma_start(w1[:, :, :], src1).then_inc(s_w1, 16)
                sp.wait_ge(s_l2, CT * e + CT)
                sp.dma_start(w2[:, :, :], src2).then_inc(s_w2, 16)
                sp.wait_ge(s_add, CT * e + CT)
                sp.dma_start(b2[:, :], srcb).then_inc(s_b2, 16)

        def pool_embed(pool, bb):
            def gather(t):
                if not (isinstance(bb, int) and bb == 0):
                    pool.wait_ge(s_h0, TS * bb + t - TS + 1)
                pool.wait_ge(s_idx, bb + 1)
                stand(pool)
                nc.gpsimd.indirect_dma_start(
                    rows[:, t, :], None, ins["tok_table"],
                    bass.IndirectOffsetOnAxis(idx_now[:, t:t + 1], 0)).then_inc(s_rows[t], 16)

            def power(t):
                pool.wait_ge(s_var0, TS * bb + t + 1)
                nc.gpsimd.tensor_tensor(out=rs0[:, t:t + 1], in0=ve0[:, t:t + 1], in1=mhalf[:, :],
                                        op=ALU.pow).then_inc(s_rs0, 1)
            return gather, power

        def pool_gather(pool, gi, q, idx, col):
            pool.wait_ge(s_fin, max(GT * gi, 1) if isinstance(gi, int) else GT * gi)
            stand(pool)
            half = (col // GT) % 2
            nc.gpsimd.indirect_dma_start(
                hrow[:, half, q, :], None, h1_rows,
                bass.IndirectOffsetOnAxis(idx[:, col:col + 1], 0)).then_inc(s_gr[q], 16)

        def pool_expert(pool, e, last):
            for g in range(GR):
                gi = GR * e + g
                if g + 1 < GR:
                    for q in range(GT):
                        pool_gather(pool, gi + 1, q, idx_next if g == 0 else idx_cur, (g + 1) * GT + q)
                elif not last:
                    pool.wait_ge(s_next, e + 2)
                    for q in range(GT):
                        pool_gather(pool, gi + 1, q, idx_next, q)
                if g > 0:
                    pool.wait_ge(s_out[1], 16 * (GT // 2 * gi))
                    pool.sem_inc(s_free, 1)
                if g + 1 < GR:
                    pool_power(pool, gi + 1)
                for q in range(GT):
                    if (g, q) == (0, 0):
                        pool.wait_ge(s_b2, 16 * e + 16)
                        pool.wait_ge(s_cur, e + 1)
                    if (g, q) == (GR - 1, 1) and not last:
                        pool_power(pool, gi + 1)
                    pool.wait_ge(s_fin, GT + GT * gi + q + 1)
                    nc.gpsimd.tensor_tensor(out=orow[:, q % 2, :], in0=orow[:, q % 2, :], in1=b2[:, :],
                                            op=ALU.add).then_inc(s_add, 1)
                    pool.wait_ge(s_add, GT * gi + q + 1)
                    stand(pool)
                    nc.gpsimd.indirect_dma_start(
                        out, bass.IndirectOffsetOnAxis(idx_cur[:, g * GT + q:g * GT + q + 1], 0),
                        orow[:, q % 2, :], None).then_inc(s_out[q % 2], 16)
                    done = ([q - 1] if q else []) + ([q] if (g, q) == (GR - 1, GT - 1) else [])
                    for r in done:
                        pool.wait_ge(s_out[r % 2], 16 * (GT // 2 * gi + r // 2 + 1))
                    if done:
                        pool.sem_inc(s_free, len(done))

        def pool_power(pool, gi):
            pool.wait_ge(s_var2, gi + 1)
            nc.gpsimd.tensor_tensor(out=rs2[:, :, :], in0=ve2[:, :, :],
                                    in1=mhalf[:, :].unsqueeze(2).to_broadcast([P, 2, GT]), op=ALU.pow).then_inc(s_rs2, 1)

        @block.gpsimd
        def _(pool):
            nc.gpsimd.memset(mhalf[:, :], -0.5).then_inc(s_mh, 1)
            pool.wait_ge(s_mh, 1)
            gather, power = pool_embed(pool, 0)
            for t in range(TS):
                gather(t)
            for t in range(TS):
                power(t)
            gather = pool_embed(pool, 1)[0]
            for t in range(TS):
                gather(t)

            def sequence(b, par):
                m = Misc(b, par)
                power = pool_embed(pool, b + 1)[1]
                gather = pool_embed(pool, b + 2)[0]
                for s in range(NUB):
                    if m.new and s in STAT_AT:
                        power(STAT_AT.index(s))
                    for task in plan[s]:
                        name, t = task
                        if name == "WO" and m.here(task):
                            pool.wait_ge(s_var1, TS * (b - lag(task)) + t + 1)
                            nc.gpsimd.tensor_tensor(out=rs1[:, :], in0=ve1[:, :], in1=mhalf[:, :],
                                                    op=ALU.pow).then_inc(s_rs1, 1)
                    if m.new and s == IDX_AT:
                        for t in range(TS):
                            gather(t)

            sequence(0, 0)
            sequence(1, 1)
            with pool.Fori(1, SEQS // 2) as i:
                sequence(2 * i, 0)
                sequence(2 * i + 1, 1)
            sequence(SEQS, 0)
            pool.wait_ge(s_h1out[0], 16 * (NT // 2 + 1))
            pool.wait_ge(s_h1out[1], 16 * (NT // 2 + 1))
            pool.wait_ge(s_next, 1)
            for q in range(GT):
                pool_gather(pool, 0, q, idx_next, q)
            pool_power(pool, 0)
            with pool.Fori(0, E - 1) as e:
                pool_expert(pool, e, False)
            pool_expert(pool, E - 1, True)
            for j in range(2):
                pool.wait_ge(s_out[j], 16 * (NT // 2))

        def act_misc(act, m, task, b, nx):
            name, t = task
            if TAKER[name] != "A" or not m.here(task):
                return
            bank = m.bank(task)
            act.wait_ge(s_misc, m.done(task))
            if name == "ET":
                if t == 0 and b is not None:
                    act.wait_ge(s_xp, b + 1)
                nc.scalar.activation(x1T[:, :, t * P:(t + 1) * P],
                                     bank[:, 0:D].rearrange("p (c n) -> p c n", c=KC), ACT.Copy).then_inc(s_mA, 1)
            elif name == "RT":
                nc.scalar.activation(remT[:, :], bank[:, 0:P], ACT.Copy).then_inc(s_mA, 1)
            elif name == "MT":
                nc.scalar.activation(mixT[:, :, :], bank[:, 0:D].rearrange("p (c n) -> p c n", c=KC),
                                     ACT.Copy).then_inc(s_mA, 1)
            elif name == "YT":
                nc.scalar.activation(yT[:, :, :], bank[:, 0:D].rearrange("p (c n) -> p c n", c=KC),
                                     ACT.Copy).then_inc(s_mA, 1)
            elif name == "Q":
                nc.scalar.activation(Qt[nx][:, t, :], bank[:, :], ACT.Copy, scale=HD ** -0.5).then_inc(s_mA, 1)
            elif name == "K":
                for j in range(2):
                    ins_ = nc.scalar.activation(Kt[nx][:, t, 1:, j, :], bank[:, :].rearrange("p (a k) -> p a k", k=W),
                                                ACT.Copy, scale=c_parity[:, j:j + 1])
                ins_.then_inc(s_mA, 1)
            elif name == "G":
                nc.scalar.activation(Gt[nx][:, :], bank[:, :], ACT.Copy, scale=HD ** -0.5).then_inc(s_mA, 1)
            elif name == "V":
                v = bank[:, 0:D].rearrange("p (h d) -> p h d", h=H)
                nc.scalar.activation(Vo[nx][:, t, :, 0:HD], v, ACT.Copy)
                nc.scalar.activation(Ve[nx][0:W, t, :, 0:HD], v[0:W, :, :], ACT.Copy)
                nc.scalar.activation(Ve[nx][W:P, t + 1, :, 0:HD], v[W:P, :, :], ACT.Copy)
                nc.scalar.activation(gt[nx][:, t, :], bank[:, D:D + 2 * H], ACT.Tanh, scale=0.5).then_inc(s_mA, 1)

        def act_rows(act, gi, q, half):
            if q == 0:
                act.wait_ge(s_scales, gi + 1)
            if q >= 2:
                act.wait_ge(s_yT, GT * gi + q - 1)
            nc.scalar.activation(y2[:, q % 2, :], hrow[:, half, q, :], ACT.Identity, scale=rs2[:, 0, q:q + 1],
                                 bias=nmr[:, 0, q:q + 1]).then_inc(s_y2, 1)
            nc.scalar.activation(hrow[:, half, q, :], hrow[:, half, q, :], ACT.Identity, scale=r1[:, q:q + 1],
                                 bias=nmr[:, 1, q:q + 1]).then_inc(s_scaled, 1)

        def act_group(act, gi, g):
            act_rows(act, gi, 0, g % 2)
            for q in range(GT):
                if q + 1 < GT:
                    act_rows(act, gi, q + 1, g % 2)
                act_transposed(act, gi, q, g)

        def act_transposed(act, gi, q, g):
            act.wait_ge(s_yT, GT * gi + q + 1)
            for c in range(KC):
                ins_ = nc.scalar.activation(hT[g % 2][:, c, q * P:(q + 1) * P], T_ps[q % 2][:, c * P:(c + 1) * P],
                                            ACT.Identity, scale=ln[:, c:c + 1], bias=ln[:, KC + c:KC + c + 1])
            ins_.then_inc(s_hT, 1)

        def act_expert(act, e, last):
            for g in range(GR):
                gi = GR * e + g
                if g == 0:
                    act.wait_ge(s_b1, e + 1)
                for m in range(FC):
                    act.wait_ge(s_l1, FC * gi + m + 1)
                    nc.scalar.activation(hid[:, m, :], S_ps[m % 2][:, 0:GT * P], ACT.Gelu_apprx_tanh,
                                         bias=b1[:, m:m + 1]).then_inc(s_hid, 1)
                if g + 1 < GR or not last:
                    act_group(act, gi + 1, g + 1 if g + 1 < GR else 0)

        @block.scalar
        def _(act):
            act.wait_ge(s_init, 3)
            nc.scalar.activation(probT[0][:, 0:P], c_ident, ACT.Copy).then_inc(s_pT, 2)
            m = Misc("head")
            for task in head_tasks:
                act_misc(act, m, task, None, 0)

            def sequence(b, par):
                m = Misc(b, par)
                for s in range(NUB):
                    at = units(s, m)
                    if at(T_LAG):
                        back, u = at(T_LAG)
                        act.wait_ge(s_T, NUB * (b - back) + u + 1)
                        nc.scalar.activation(probT[u % 2][:, :], T_ps[u % 2][:, :], ACT.Copy).then_inc(s_pT, 1)
                    if m.new:
                        act.wait_ge(s_shift, 2 + NUB * b + s + 1)
                        nc.scalar.activation(prob[:, s % RING, :], prob[:, s % RING, :], ACT.Exp).then_inc(s_exp, 1)
                    for task in plan[s]:
                        act_misc(act, m, task, b, 1 - par)

            sequence(0, 0)
            sequence(1, 1)
            with act.Fori(1, SEQS // 2) as i:
                sequence(2 * i, 0)
                sequence(2 * i + 1, 1)
            sequence(SEQS, 0)
            nc.scalar.activation(probT[0][:, 0:P], c_ident, ACT.Copy).then_inc(s_hid, 2)
            act_group(act, 0, 0)
            with act.Fori(0, E - 1) as e:
                act_expert(act, e, False)
            act_expert(act, E - 1, True)

        def pe_misc(pe, m, task, b):
            name, t = task
            if not m.here(task):
                return
            bb = 0 if b is None else b + 1
            bt = None if b is None else b - lag(task)
            bank = m.bank(task)
            m.free(pe, task)
            if name == "ET":
                pe.wait_ge(s_xn, TS * bb + t + 1)
                for c in range(KC):
                    mm = nc.tensor.transpose(bank[:, c * P:(c + 1) * P], xn[:, t % 2, c * P:(c + 1) * P], c_ident)
            elif name == "RT":
                pe.wait_ge(s_rem, TS * bt + t + 1)
                mm = nc.tensor.transpose(bank[:, 0:P], rem[:, :, :].rearrange("p h d -> p (h d)"), c_ident)
            elif name == "RO":
                pe.wait_ge(s_mA, m.out(("RT", t), task))
                mm = nc.tensor.matmul(bank[:, 0:D], remT[:, :], wro[:, :], start=True, stop=True)
            elif name == "MT":
                pe.wait_ge(s_mix, TS * bt + t + 1)
                for c in range(KC):
                    mm = nc.tensor.transpose(bank[:, c * P:(c + 1) * P], mix[:, c * P:(c + 1) * P], c_ident)
            elif name == "WO":
                pe.wait_ge(s_mA, m.out(("MT", t), task))
                for c in range(KC):
                    mm = nc.tensor.matmul(bank[:, 0:D], mixT[:, c, :], wout[:, c, :], start=c == 0, stop=c == KC - 1)
            elif name == "YT":
                pe.wait_ge(s_y, TS * bt + t + 1)
                for c in range(KC):
                    mm = nc.tensor.transpose(bank[:, c * P:(c + 1) * P], y[:, c * P:(c + 1) * P], c_ident)
            elif name == "SC":
                pe.wait_ge(s_mA, m.out(("YT", t), task))
                for c in range(KC):
                    mm = nc.tensor.matmul(bank[:, 0:E], yT[:, c, :], cenT[:, c, :], start=c == 0, stop=c == KC - 1)
            elif name in "QKG":
                if (name, t) == ("Q", 0):
                    pe.wait_ge(s_mA, m.out(("ET", TS - 1)))
                w = {"Q": wq, "K": wk, "G": wgq}[name]
                for c in range(KC):
                    mm = nc.tensor.matmul(bank[:, :], w[:, c, t * P:(t + 1) * P], x1T[:, c, :],
                                          start=c == 0, stop=c == KC - 1)
            elif name == "PK":
                pe.wait_ge(s_xp, bb + 1)
                for c in range(KC):
                    mm = nc.tensor.matmul(bank[:, 0:NL], wgk[:, c, :], xp[:, c, 0, :], start=c == 0, stop=c == KC - 1)
            elif name == "PV":
                for c in range(KC):
                    mm = nc.tensor.matmul(bank[:, 0:LD], xp[:, c, :, :].rearrange("p a n -> p (a n)"), wgv[:, c, :],
                                          start=c == 0, stop=c == KC - 1)
            elif name == "V":
                for c in range(KC):
                    mm = nc.tensor.matmul(bank[:, 0:D + 2 * H], x1T[:, c, t * P:(t + 1) * P], wvg[:, c, :],
                                          start=c == 0, stop=c == KC - 1)
            mm.then_inc(s_misc, 1)

        LPS = M_ps[1][:, 0:CT]

        def pe_choice(pe, n, part, k):
            if part == "radix":
                pe.wait_ge(s_cand, DIGITS * n + k + 1)
                nc.tensor.matmul(M_ps[0][:, 0:RADIX - 1], onesb[:, :], counts[:, :], start=True, stop=True)\
                    .then_inc(s_total, 1)
            elif part == "ties":
                pe.wait_ge(s_cut, n + 1)
                nc.tensor.matmul(M_ps[0][:, 0:NT], beforeb[:, :], equal[:, :], start=True, stop=True)
                nc.tensor.matmul(M_ps[0][:, P:P + NT], onesb[:, :], equal[:, :], start=True, stop=True)
                nc.tensor.matmul(M_ps[0][:, 2 * P:2 * P + 1], onesb[:, :], nabove[:, :], start=True, stop=True)\
                    .then_inc(s_ties, 1)
            elif part == "pos":
                pe.wait_ge(s_sel, n + 1)
                nc.tensor.matmul(M_ps[0][:, 0:NT], beforeb[:, :], chosenb[:, :], start=True, stop=True)
                nc.tensor.matmul(M_ps[0][:, P:P + NT], onesb[:, :], chosenb[:, :], start=True, stop=True)\
                    .then_inc(s_pos, 1)
            elif part == "list":
                if k == 0:
                    pe.wait_ge(s_ohA, n + 1)
                pe.wait_ge(s_ohB, LC * n + k + 1)
                for j in range(LT):
                    for half in (ohP, ohT):
                        first_, last_ = k == 0 and j == 0 and half is ohP, k == LC - 1 and j == LT - 1 and half is ohT
                        mm = nc.tensor.matmul(LPS, ohB[:, k % 2, j, :], half[:, k * LT + j, :],
                                              start=first_, stop=last_)
                mm.then_inc(s_used, 1)

        assert GR == 4 and DIGITS == 8 and LC == 8 and FC == 8 and GT == 4
        Q0 = FC
        pe_at = {(2, 1): [("ties", 0)], (2, 3): [("pos", 0)],
                 (2, Q0 + 1): [("list", 0)], (2, Q0 + 2): [("list", 1)], (2, Q0 + 3): [("list", 2)],
                 (3, 0): [("list", 3)], (3, 1): [("list", 4)], (3, 2): [("list", 5)], (3, 3): [("list", 6)],
                 (3, 5): [("list", 7)]}
        dve_at = {(2, 0): [("digit", 7), ("cut", 0)], (2, 2): [("ties", 0)], (2, 4): [("pos", 0)],
                  (2, 5): [("stats", 0)], (2, 6): [("list", 0)], (2, 7): [("scales", 0)], (2, Q0): [("places", 0)],
                  (2, Q0 + 1): [("list", 1)], (2, Q0 + 2): [("list", 2)], (2, Q0 + 3): [("list", 3)],
                  (3, 0): [("list", 4), ("list", 5), ("list", 6), ("list", 7), ("numbers", 0)],
                  (3, Q0 + 1): [("stats", 0)], (3, Q0 + 2): [("scales", 0)]}
        for g in range(2):
            for n, slot in enumerate((2, 5, Q0 + 1, Q0 + 3)):
                pe_at[g, slot] = [("radix", 4 * g + n)]
            dve_at[g, 0] = [("digit", 3)] * g + [("count", 4 * g)]
            dve_at[g, 3] = [("numbers now", 0)] * (g == 0) + [("digit", 4 * g), ("count", 4 * g + 1)]
            dve_at[g, 5] = [("stats", 0)]
            dve_at[g, 6] = [("digit", 4 * g + 1)]
            dve_at[g, 7] = [("scales", 0)]
            dve_at[g, Q0] = [("count", 4 * g + 2)]
            dve_at[g, Q0 + 2] = [("digit", 4 * g + 2), ("count", 4 * g + 3)]
        PE_PARTS = [("radix", k) for k in range(DIGITS)] + [("ties", 0), ("pos", 0)] + [("list", k) for k in range(LC)]
        DVE_PARTS = [(x, k) for k in range(DIGITS) for x in ("count", "digit")] + \
            [(x, 0) for x in ("cut", "ties", "pos", "places")] + [("list", k) for k in range(LC)] + [("numbers", 0)]

        def pe_rows(pe, gi, q):
            pe.wait_ge(s_y2, GT * gi + q + 1)
            if q >= 2:
                pe.wait_ge(s_hT, GT * gi + q - 1)
            else:
                pe.wait_ge(s_hid, 2)
            for c in range(KC):
                mm = nc.tensor.transpose(T_ps[q % 2][:, c * P:(c + 1) * P], y2[:, q % 2, c * P:(c + 1) * P], c_ident)
            mm.then_inc(s_yT, 1)

        def pe_expert(pe, e, last):
            for g in range(GR):
                gi = GR * e + g
                for m in range(FC):
                    if m == 0:
                        pe.wait_ge(s_hT, GT * gi + GT)
                        if g == 0:
                            pe.wait_ge(s_w1, 16 * e + 16)
                    pe.wait_ge(s_hid, FC * gi + m + 1)
                    for c in range(KC):
                        mm = nc.tensor.matmul(S_ps[m % 2][:, 0:GT * P], w1[:, c, m * P:(m + 1) * P], hT[g % 2][:, c, :],
                                              start=c == 0, stop=c == KC - 1)
                    mm.then_inc(s_l1, 1)
                    if not last:
                        for part, k in pe_at.get((g, m), []):
                            pe_choice(pe, e + 1, part, k)
                for q in range(GT):
                    if q == 0 and g == 0:
                        pe.wait_ge(s_w2, 16 * e + 16)
                    pe.wait_ge(s_fin, GT + GT * gi + q - 1)
                    for m in range(FC):
                        if q == 0 and m >= FC - 2:
                            pe.wait_ge(s_hid, 2 + FC * gi + m + 1)
                        mm = nc.tensor.matmul(O_ps[q % 2][:, 0:D], hid[:, m, q * P:(q + 1) * P], w2[:, m, :],
                                              start=m == 0, stop=m == FC - 1)
                    mm.then_inc(s_l2, 1)
                    if not last:
                        for part, k in pe_at.get((g, FC + q), []):
                            pe_choice(pe, e + 1, part, k)
                    if g + 1 < GR:
                        for r in ([0, 1], [2], [3], [])[q]:
                            pe_rows(pe, gi + 1, r)
                    elif not last:
                        for r in ([], [], [0, 1], [2, 3])[q]:
                            pe_rows(pe, gi + 1, r)

        @block.tensor
        def _(pe):
            pe.wait_ge(s_load, 16 * LOADS)
            pe.wait_ge(s_init, 3)
            for t in range(TS):
                nc.tensor.transpose(M_ps[0][:, t * SEQS:(t + 1) * SEQS], xw[:, t * P:(t + 1) * P],
                                    c_ident[0:SEQS, 0:SEQS])
                nc.tensor.transpose(M_ps[0][:, (TS + t) * SEQS:(TS + t + 1) * SEQS], xs[:, t * P:(t + 1) * P],
                                    c_ident[0:SEQS, 0:SEQS])
            for c in range(KC):
                mm = nc.tensor.transpose(M_ps[1][:, c * E:(c + 1) * E], cen[:, c * P:(c + 1) * P], c_ident[0:E, 0:E])
            nc.tensor.transpose(M_ps[1][:, 128:128 + E * FC], b1_rows[:, :], c_ident[0:E * FC, 0:E * FC])
            mm = nc.tensor.transpose(M_ps[1][:, 32:32 + 2 * KC], ln_rows[:, :], c_ident[0:2 * KC, 0:2 * KC])
            mm.then_inc(s_setT, 1)
            pe.wait_ge(s_setE, 2)
            for c in range(KC):
                mm = nc.tensor.matmul(M_ps[1][:, 64:64 + E], lnb_row[:, c, :], cenT[:, c, :],
                                      start=c == 0, stop=c == KC - 1)
            mm.then_inc(s_setT, 1)
            pe.wait_ge(s_setE, 4)
            m = Misc("head")
            for task in head_tasks:
                pe_misc(pe, m, task, None)

            def scores(b, par, s):
                t, g = divmod(s, NU)
                bank = S_ps[s % 2]
                pe.wait_ge(s_shift, NUB * b + s + 1)
                if g < H // G:
                    nc.tensor.matmul(bank[:, :].rearrange("p (g k) -> p g k", g=G), identb[:, :],
                                     band[:, min(t, 1), :].unsqueeze(1).to_broadcast([P, G, P]),
                                     start=True, stop=False)
                    cols = bank[:, :].rearrange("p (h a k) -> p h a k", h=G, a=2)
                    for n in range(0, G, 2):
                        c, r = unit_head(g, n) // 8, 32 * g
                        for a, lo, hi, block in ((0, 0, P, 2 * t + 1), (1, 0, W, 2 * t), (1, W, P, 2 * t + 2)):
                            mm = nc.tensor.matmul(cols[lo:hi, n:n + 2, a, :],
                                                  Qt[par][r:r + 32, c, t * P + lo:t * P + hi],
                                                  Kt[par][r:r + 32, c, block, :, :],
                                                  start=False, stop=n == G - 2 and a == 1)
                else:
                    nc.tensor.matmul(bank[:, :].rearrange("p (h n) -> p h n", h=LH), identb[:, :],
                                     latm[:, t, :].unsqueeze(1).to_broadcast([P, LH, NL]),
                                     start=True, stop=False)
                    mm = nc.tensor.matmul(bank[:, :], Gt[par][:, t * P:(t + 1) * P],
                                          bdK[par][:, :, :].rearrange("p h n -> p (h n)"), start=False, stop=True)
                mm.then_inc(s_S, 1)

            def values(b, par, u):
                t, g = divmod(u, NU)
                if g == 0:
                    pe.wait_ge(s_O, TS * b + t + 1)
                pe.wait_ge(s_pT, 2 + NUB * b + u + 1)
                for n in range(G):
                    if g < H // G:
                        h = unit_head(g, n)
                        for q, vals in ((0, Ve[par]), (1, Vo[par])):
                            mm = nc.tensor.matmul(
                                O_ps[t % 2][W * q:W * (q + 1), h * OW:(h + 1) * OW],
                                probT[u % 2][:, n * P + W * q:n * P + W * (q + 1)],
                                vals[:, t, h, :], start=True, stop=True)
                    else:
                        c = (H + 2 * n) * OW
                        mm = nc.tensor.matmul(O_ps[t % 2][:, c:c + 2 * OW], probT[u % 2][:, n * P:(n + 1) * P],
                                              bdV[par][:, n, :, :].rearrange("p a d -> p (a d)"),
                                              start=True, stop=True)
                mm.then_inc(s_PV, 1)

            def sequence(b, par):
                m = Misc(b, par)
                if m.new:
                    pe.wait_ge(s_mA, m.out_before(("V", TS - 1)))
                    pe.wait_ge(s_mD, m.out_before(("PV", 0)))
                for s in range(NUB):
                    at = units(s, m)
                    if m.new:
                        scores(b, par, s)
                    if at(T_LAG):
                        back, u = at(T_LAG)
                        pe.wait_ge(s_exp, NUB * (b - back) + u + 1)
                        pe.wait_ge(s_pT, NUB * (b - back) + u + 1)
                        for n in range(G):
                            mm = nc.tensor.transpose(T_ps[u % 2][:, n * P:(n + 1) * P],
                                                     prob[:, u % RING, n * P:(n + 1) * P], c_ident)
                        mm.then_inc(s_T, 1)
                    if at(O_LAG):
                        back, u = at(O_LAG)
                        values(b - back, (par + back) % 2, u)
                    for task in plan[s]:
                        pe_misc(pe, m, task, b)

            sequence(0, 0)
            sequence(1, 1)
            with pe.Fori(1, SEQS // 2) as i:
                sequence(2 * i, 0)
                sequence(2 * i + 1, 1)
            sequence(SEQS, 0)
            pe.wait_ge(s_mA, Misc(SEQS).end("A"))
            pe.wait_ge(s_mD, Misc(SEQS).end("D"))
            for part, k in PE_PARTS:
                pe_choice(pe, 0, part, k)
            for q in range(GT):
                pe_rows(pe, 0, q)
            with pe.Fori(0, E - 1) as e:
                pe_expert(pe, e, False)
            pe_expert(pe, E - 1, True)

        CH = {"n": 0}

        def chain(dve, ins_, base=0):
            CH["n"] += 1
            ins_.then_inc(s_v, 1)
            dve.wait_ge(s_v, base + CH["n"])

        def dve_indices(dve, bb):
            nc.vector.tensor_copy(seg_now[:, :].unsqueeze(2), seg_all[:, :, bass.ds(bb, 1)])
            nc.vector.tensor_copy(idx_now[:, :].unsqueeze(2), idx_all[:, :, bass.ds(bb, 1)]).then_inc(s_idx, 1)
            dve.wait_ge(s_idx, bb + 1)

        def dve_embed(dve, m, bb, par, base):

            def res(t):
                return hres[:, par, t, :]

            def embed(t):
                dve.wait_ge(s_rows[t], 16 * bb + 16)
                chain(dve, nc.vector.scalar_tensor_tensor(out=res(t), in0=rows[:, t, :], scalar=float(D) ** 0.5,
                                                          in1=P16[:, t, :], op0=ALU.mult, op1=ALU.add), base)
                nc.vector.scalar_tensor_tensor(out=res(t), in0=D16[:, :], scalar=seg_now[:, t:t + 1],
                                               in1=res(t), op0=ALU.mult, op1=ALU.add).then_inc(s_h0, 1)

            def stats(t):
                dve.wait_ge(s_h0, TS * bb + t + 1)
                stand(dve)
                chain(dve, nc.vector.bn_stats(st0[:, :], res(t)), base)
                stand(dve)
                chain(dve, nc.vector.bn_aggr(mv0[:, t, :], st0[:, :]), base)
                nc.vector.tensor_scalar(ve0[:, t:t + 1], mv0[:, t, 1:2], EPS, None, ALU.add).then_inc(s_var0, 1)

            def norm(t):
                if t >= 2:
                    dve.wait_ge(s_misc, m.done(("ET", t - 2)))
                dve.wait_ge(s_rs0, TS * bb + t + 1)
                nc.vector.tensor_scalar(xn[:, t % 2, :], res(t), mv0[:, t, 0:1], rs0[:, t:t + 1],
                                        ALU.subtract, ALU.mult).then_inc(s_xn, 1)

            def pool_latents():
                dve.wait_ge(s_mA, m.out(("ET", TS - 1)))
                chain(dve, nc.vector.tensor_reduce(
                    xp[:, :, 0, :], x1T[:, :, :].rearrange("p c (n k) -> p c n k", n=NL), AX.X, ALU.add), base)
                nc.vector.tensor_copy(xp[:, :, 1, :], xp[:, :, 0, :]).then_inc(s_xp, 1)
            return embed, stats, norm, pool_latents

        def dve_misc(dve, m, task, b, nx, base):
            name, t = task
            bt = None if b is None else b - lag(task)
            if TAKER[name] != "D" or not m.here(task):
                return
            bank = m.bank(task)
            dve.wait_ge(s_misc, m.done(task))
            if name == "PK":
                nc.vector.tensor_tensor(bdK[nx][:, :, :], bank[:, 0:NL].unsqueeze(1).to_broadcast([P, LH, NL]),
                                        c_own.unsqueeze(2).to_broadcast([P, LH, NL]), ALU.mult).then_inc(s_mD, 1)
            elif name == "PV":
                for r in range(2):
                    ins_ = nc.vector.tensor_scalar(
                        bdV[nx][NL * r:NL * (r + 1), :, r, 0:HD],
                        bank[NL * r:NL * (r + 1), 0:LD].rearrange("p (a r d) -> p a r d", r=2, d=HD)[:, :, r, :],
                        float(NL) / S, None, ALU.mult)
                ins_.then_inc(s_mD, 1)
            elif name == "RO":
                nc.vector.tensor_tensor(r2[:, :, :], bank[:, 0:D].rearrange("p (h d) -> p h d", h=H),
                                        sg[:, H:2 * H].unsqueeze(2).to_broadcast([P, H, HD]), ALU.mult).then_inc(s_mD, 1)
                dve.wait_ge(s_mD, m.out(task))
                nc.vector.tensor_tensor(mix[:, :].rearrange("p (h d) -> p h d", h=H), loc[:, :, :], r2[:, :, :],
                                        ALU.add).then_inc(s_mix, 1)
            elif name == "WO":
                dve.wait_ge(s_h1out[t % 2], 16 * (TS // 2 * bt + t // 2) + 16)
                nc.vector.tensor_tensor(h1[:, t % 2, :],
                                        hres[:, (1 - nx + lag(task)) % 2, t, :],
                                        bank[:, 0:D], ALU.add).then_inc(s_mD, 1)
                dve.wait_ge(s_mD, m.out(task))
                chain(dve, nc.vector.bn_stats(st1[:, :], h1[:, t % 2, :]), base)
                stand(dve)
                chain(dve, nc.vector.bn_aggr(mv1[:, :], st1[:, :]), base)
                nc.vector.tensor_scalar(ve1[:, :], mv1[:, 1:2], 1.0 + EPS, EPS * EPS, ALU.mult, ALU.add)\
                    .then_inc(s_var1, 1)
            elif name == "SC":
                nc.vector.tensor_tensor(score[:, :, bass.ds(TS * bt + t, 1)], bank[:, 0:E].unsqueeze(2),
                                        kb[:, :].unsqueeze(2), ALU.add).then_inc(s_mD, 1)

        def dve_outputs(dve, b, par, t, base):
            O = O_ps[t % 2][:, 0:(H + LH) * OW].rearrange("p (h d) -> p h d", d=OW)
            dve.wait_ge(s_PV, NUB * b + NU * (t + 1))
            nc.vector.tensor_scalar(sg[:, :], gt[par][:, t, :], 0.5, 0.5, ALU.mult, ALU.add)
            chain(dve, nc.vector.reciprocal(rc[:, :].unsqueeze(2), O[:, :, HD:OW]), base)
            nc.vector.tensor_tensor(rem[:, :, :], O[:, H:, 0:HD],
                                    rc[:, H:].unsqueeze(2).to_broadcast([P, LH, HD]), ALU.mult).then_inc(s_rem, 1)
            chain(dve, nc.vector.tensor_tensor(cl[:, :], rc[:, 0:H], sg[:, 0:H], ALU.mult), base)
            nc.vector.tensor_tensor(loc[:, :, :], O[:, 0:H, 0:HD],
                                    cl[:, :].unsqueeze(2).to_broadcast([P, H, HD]), ALU.mult).then_inc(s_O, 1)

        def dve_as_float(dve, src, dst, width, base):
            chain(dve, nc.vector.tensor_scalar(flip[:, 0:width], src, 31, -1 << 31,
                                               ALU.arith_shift_right, ALU.bitwise_or), base)
            chain(dve, nc.vector.scalar_tensor_tensor(out=dst, in0=src, scalar=0x7FFFFFFF, in1=flip[:, 0:width],
                                                      op0=ALU.bitwise_xor, op1=ALU.bitwise_xor), base)

        def dve_choice(dve, n, part, k, base):
            if part == "count":
                if k == 0:
                    chain(dve, nc.vector.scalar_tensor_tensor(
                        out=act_s[:, :].unsqueeze(1), in0=taken[:, :].unsqueeze(1), scalar=TAKEN,
                        in1=score[:, bass.ds(n, 1), :], op0=ALU.mult, op1=ALU.add), base)
                    chain(dve, nc.vector.memset(thr[:, :], 0), base)
                chain(dve, nc.vector.tensor_tensor(cand[:, :], digits[:, k, :],
                                                   thr[:, :].to_broadcast([P, RADIX - 1]), ALU.bitwise_or), base)
                dve_as_float(dve, cand[:, :], cval[:, :], RADIX - 1, base)
                for c in range(RADIX - 1):
                    ins_ = nc.vector.tensor_scalar(hits[:, c, :], act_s[:, :], cval[:, c:c + 1].bitcast(F32), None,
                                                   ALU.is_ge, ALU.add, accum_out=counts[:, c:c + 1])
                ins_.then_inc(s_cand, 1)
            elif part == "digit":
                dve.wait_ge(s_total, DIGITS * n + k + 1)
                chain(dve, nc.vector.tensor_scalar(over[:, :], M_ps[0][:, 0:RADIX - 1], float(C), None,
                                                   ALU.is_ge, ALU.add, accum_out=nover[:, :]), base)
                chain(dve, nc.vector.tensor_scalar(delta[:, :], nover[:, :], float(2 ** (32 - BITS * (k + 1))), None,
                                                   ALU.mult), base)
                chain(dve, nc.vector.tensor_tensor(thr[:, :], thr[:, :], delta[:, :].bitcast(I32),
                                                   ALU.bitwise_or), base)
            elif part == "cut":
                dve_as_float(dve, thr[:, :], cval[:, 0:1], 1, base)
                T_ = cval[:, 0:1].bitcast(F32)
                chain(dve, nc.vector.tensor_scalar(above[:, :], act_s[:, :], T_, None, ALU.is_gt, ALU.add,
                                                   accum_out=nabove[:, :]), base)
                nc.vector.tensor_scalar(equal[:, :], act_s[:, :], T_, None, ALU.is_equal).then_inc(s_cut, 1)
            elif part == "ties":
                dve.wait_ge(s_ties, n + 1)
                chain(dve, nc.vector.tensor_scalar(need[:, :], M_ps[0][:, 2 * P:2 * P + 1], -1.0, float(C),
                                                   ALU.mult, ALU.add), base)
                dve_prefix(dve, base)
                chain(dve, nc.vector.scalar_tensor_tensor(out=chosen[:, :], in0=rank[:, :], scalar=need[:, :],
                                                          in1=equal[:, :], op0=ALU.is_lt, op1=ALU.mult), base)
                chain(dve, nc.vector.tensor_tensor(chosen[:, :], chosen[:, :], above[:, :], ALU.add), base)
                nc.vector.tensor_tensor(taken[:, :], taken[:, :], chosen[:, :], ALU.add)
                nc.vector.tensor_copy(chosenb[:, :], chosen[:, :]).then_inc(s_sel, 1)
                dve.wait_ge(s_sel, n + 1)
            elif part == "pos":
                dve.wait_ge(s_pos, n + 1)
                dve_prefix(dve, base)
                chain(dve, nc.vector.tensor_copy(ranki[:, :], rank[:, :]), base)
                chain(dve, nc.vector.tensor_scalar(rlowi[:, :], ranki[:, :], P - 1, None, ALU.bitwise_and), base)
                chain(dve, nc.vector.tensor_scalar(ranki[:, :], ranki[:, :], 7, None, ALU.arith_shift_right), base)
                chain(dve, nc.vector.tensor_copy(rhigh[:, :], ranki[:, :]), base)
                chain(dve, nc.vector.scalar_tensor_tensor(out=rlow[:, :], in0=rlowi[:, :], scalar=1.0,
                                                          in1=chosen[:, :], op0=ALU.add, op1=ALU.mult), base)
                chain(dve, nc.vector.tensor_scalar(rlow[:, :], rlow[:, :], -1.0, None, ALU.add), base)
            elif part == "places":
                chain(dve, nc.vector.tensor_tensor(ohA[:, :, :], rhigh[:, :].unsqueeze(2).to_broadcast([P, NT, CT]),
                                                   laneb[:, 0:CT].unsqueeze(1).to_broadcast([P, NT, CT]),
                                                   ALU.is_equal), base)
                nc.vector.tensor_scalar(ohP[:, :, :], ohA[:, :, :], c_part, None, ALU.mult)
                nc.vector.scalar_tensor_tensor(out=ohT[:, :, :], in0=ohA[:, :, :], scalar=float(P),
                                               in1=laneb[:, 0:NT].unsqueeze(2).to_broadcast([P, NT, CT]),
                                               op0=ALU.mult, op1=ALU.mult).then_inc(s_ohA, 1)
            elif part == "list":
                if not (isinstance(n, int) and k < 2):
                    dve.wait_ge(s_used, LC * n + k - 1)
                nc.vector.tensor_tensor(ohB[:, k % 2, :, :], laneb[:, :].unsqueeze(1).to_broadcast([P, LT, P]),
                                        rlow[:, k * LT:(k + 1) * LT].unsqueeze(2).to_broadcast([P, LT, P]),
                                        ALU.is_equal).then_inc(s_ohB, 1)
            elif part == "numbers":
                dve.wait_ge(s_used, LC * n + LC)
                nc.vector.tensor_copy(idx_next[:, :], LPS).then_inc(s_next, 1)

        def dve_prefix(dve, base):
            totals = M_ps[0][:, P:P + NT]
            chain(dve, nc.vector.tensor_copy(rank[:, :], totals), base)
            chain(dve, nc.vector.tensor_tensor_scan(cum[:, :], rank[:, :], zeros[:, :], 0.0, ALU.add, ALU.add), base)
            chain(dve, nc.vector.tensor_tensor(cum[:, :], cum[:, :], rank[:, :], ALU.subtract), base)
            chain(dve, nc.vector.tensor_tensor(rank[:, :], cum[:, :], M_ps[0][:, 0:NT], ALU.add), base)

        def dve_stats(dve, gi, half, base):
            if not (isinstance(gi, int) and gi == 0):
                dve.wait_ge(s_scaled, GT * gi)
            for q in range(GT):
                dve.wait_ge(s_gr[q], 16 * gi + 16)
                nc.vector.bn_stats(st2[:, q, :], hrow[:, half, q, :])
            chain(dve, nc.vector.memset(r1[:, :], 1.0), base)
            stand(dve)
            for q in range(GT):
                ins_ = nc.vector.bn_aggr(mv2[:, q, :], st2[:, q, :])
            chain(dve, ins_, base)
            nc.vector.tensor_scalar(ve2[:, 0, :].unsqueeze(2), mv2[:, :, 1:2], 1.0 + EPS, EPS * EPS, ALU.mult, ALU.add)
            nc.vector.tensor_scalar(ve2[:, 1, :].unsqueeze(2), mv2[:, :, 1:2], EPS, None, ALU.add).then_inc(s_var2, 1)

        def dve_scales(dve, gi, base):
            dve.wait_ge(s_rs2, gi + 1)
            nc.vector.tensor_scalar(r1[:, :], rs2[:, 1, :], 1.0, None, ALU.add)
            nc.vector.scalar_tensor_tensor(out=nmr[:, :, :], in0=mv2[:, :, 0].unsqueeze(1).to_broadcast([P, 2, GT]),
                                           scalar=-1.0, in1=rs2[:, :, :], op0=ALU.mult, op1=ALU.mult)\
                .then_inc(s_scales, 1)

        def dve_expert(dve, e, last, base):
            dve.wait_ge(s_hid, 2 + FC * GR * e)
            nc.vector.tensor_copy(b1[:, :].unsqueeze(1), b1_all[:, bass.ds(e, 1), :]).then_inc(s_b1, 1)
            for g in range(GR):
                gi = GR * e + g
                more = g + 1 < GR or not last

                def parts(slot):
                    for part, k in dve_at.get((g, slot), []):
                        if part == "stats":
                            if more:
                                dve_stats(dve, gi + 1, (g + 1) % 2, base)
                        elif part == "scales":
                            if more:
                                dve_scales(dve, gi + 1, base)
                        elif part == "numbers now":
                            dve.wait_ge(s_free, 2 + CT * e)
                            nc.vector.tensor_copy(idx_cur[:, :], idx_next[:, :]).then_inc(s_cur, 1)
                        elif not last:
                            dve_choice(dve, e + 1, part, k, base)

                for m in range(FC):
                    parts(m)
                for q in range(GT):
                    parts(FC + q)
                    dve.wait_ge(s_l2, GT * gi + q + 1)
                    dve.wait_ge(s_scaled, GT * gi + q + 1)
                    dve.wait_ge(s_free, GT * gi + q + 1)
                    nc.vector.tensor_tensor(orow[:, q % 2, :], O_ps[q % 2][:, 0:D], hrow[:, g % 2, q, :],
                                            ALU.add).then_inc(s_fin, 1)

        @block.vector
        def _(dve):
            dve.wait_ge(s_load, 16 * LOADS)
            chain(dve, nc.vector.tensor_copy(xf[:, :], xi[:, :]))
            chain(dve, nc.vector.tensor_scalar(xw[:, :], xf[:, :], 0.0, float(V), ALU.is_lt, ALU.mult))
            chain(dve, nc.vector.tensor_tensor(xw[:, :], xw[:, :], xf[:, :], ALU.add))
            chain(dve, nc.vector.tensor_scalar(xw[:, :], xw[:, :], 0.0, float(V - 1), ALU.max, ALU.min))
            chain(dve, nc.vector.tensor_scalar(xf[:, :], xf[:, :], float(SEP), None, ALU.is_equal))
            nc.vector.tensor_tensor_scan(xs[:, :], xf[:, :], xf[:, :], 0.0, ALU.max, ALU.max).then_inc(s_init, 1)
            nc.vector.tensor_copy(identb[:, :], c_ident)
            nc.vector.tensor_copy(beforeb[:, :], c_before)
            nc.vector.tensor_copy(laneb[:, :], c_lane)
            nc.vector.memset(onesb[:, :], 1.0)
            nc.vector.memset(taken[:, :], 0.0)
            nc.vector.memset(zeros[:, :], 0.0)
            nc.vector.tensor_copy(band[:, :, :].rearrange("p a k -> p (a k)"), c_band)
            nc.vector.tensor_copy(latm[:, :, :].rearrange("p a k -> p (a k)"), c_lat)
            for par in range(2):
                nc.vector.memset(Kt[par][:, :, 0, :, :], 0.0)
                nc.vector.memset(Vo[par][:, :, :, HD:OW], 1.0)
                chain(dve, nc.vector.memset(Ve[par][:, :, :, :], 0.0))
                nc.vector.memset(Ve[par][:, :, :, HD:OW], 1.0)
                chain(dve, nc.vector.memset(bdV[par][:, :, :, :], 0.0))
                nc.vector.memset(bdV[par][0:NL, :, 0, HD:OW], 1.0)
                nc.vector.memset(bdV[par][NL:P, :, 1, HD:OW], 1.0)
            chain(dve, nc.vector.tensor_tensor(P16[:, :, :], P16[:, :, :],
                                               segs[:, 0:1, :].to_broadcast([P, TS, D]), ALU.add))
            chain(dve, nc.vector.tensor_tensor(D16[:, :], segs[:, 1, :], segs[:, 0, :], ALU.subtract))
            chain(dve, nc.vector.tensor_scalar(P16[:, :, :], P16[:, :, :], float(D) ** 0.5, None, ALU.mult))
            chain(dve, nc.vector.tensor_scalar(D16[:, :], D16[:, :], float(D) ** 0.5, None, ALU.mult))
            for j in range(2):
                chain(dve, nc.vector.tensor_tensor(gprod[:, :, j, :], wq[:, :, :],
                                                   gates[:, j:j + 1, :].to_broadcast([P, KC, D]), ALU.mult))
                nc.vector.tensor_reduce(wvg[:, :, D + H * j:D + H * (j + 1)],
                                        gprod[:, :, j, :].rearrange("p c (h d) -> p c h d", h=H), AX.X, ALU.add)
            nc.vector.memset(mx[:, :, :], 0.0).then_inc(s_init, 2)
            dve.wait_ge(s_setT, 1)
            nc.vector.tensor_copy(idx_all[:, :, 0:SEQS], M_ps[0][:, 0:TS * SEQS].rearrange("p (t b) -> p t b", t=TS))
            numbers = M_ps[0][:, 0:TS * SEQS].rearrange("p (t b) -> p t b", t=TS)[:, :, 0:1]
            nc.vector.tensor_copy(idx_all[:, :, SEQS:SEQS + 2], numbers.to_broadcast([P, TS, 2]))
            nc.vector.memset(seg_all[:, :, SEQS:SEQS + 2], 0.0)
            nc.vector.tensor_copy(seg_all[:, :, 0:SEQS],
                                  M_ps[0][:, TS * SEQS:2 * TS * SEQS].rearrange("p (t b) -> p t b", t=TS))
            for c in range(KC):
                nc.vector.tensor_copy(lnb_row[:, c, :], M_ps[1][:, 32 + KC + c:33 + KC + c].to_broadcast([P, P]))
            nc.vector.tensor_copy(ln[:, :], M_ps[1][:, 32:32 + 2 * KC])
            nc.vector.tensor_copy(b1_all[:, :, :], M_ps[1][:, 128:128 + E * FC].rearrange("p (e m) -> p e m", e=E))
            nc.vector.tensor_copy(cenT[:, :, :], M_ps[1][:, 0:KC * E].rearrange("p (c e) -> p c e", c=KC))\
                .then_inc(s_setE, 2)
            dve.wait_ge(s_setT, 2)
            nc.vector.tensor_copy(kb[:, :], M_ps[1][:, 64:64 + E])
            nc.vector.tensor_tensor(cenT[:, :, :], cenT[:, :, :],
                                    ln[:, 0:KC].unsqueeze(2).to_broadcast([P, KC, E]), ALU.mult).then_inc(s_setE, 2)
            dve.wait_ge(s_setE, 4)
            nc.vector.memset(mx[:, :, :], 0.0).then_inc(s_shift, 2)
            nc.vector.memset(st0[:, :], 0.0).then_inc(s_O, 2)
            nc.vector.memset(st1[:, :], 0.0).then_inc(s_h1out[0], 16)
            nc.vector.memset(mv1[:, :], 0.0).then_inc(s_h1out[1], 16)

            m = Misc("head")
            embed, stats, norm, pool_latents = dve_embed(dve, m, 0, 0, 0)
            dve_indices(dve, 0)
            for t in range(TS):
                embed(t)
                stats(t)
            for t in range(TS):
                norm(t)
            dve_indices(dve, 1)
            pool_latents()
            for task in head_tasks:
                dve_misc(dve, m, task, None, 0, 0)

            def sequence(b, par, base):
                m = Misc(b, par)
                embed, stats, norm, pool_latents = dve_embed(dve, m, b + 1, 1 - par, base)
                for s in range(NUB):
                    if m.new:
                        g = s % NU
                        heads = G if g < H // G else LH
                        sc = S_ps[s % 2][:, :].rearrange("p (h k) -> p h k", h=heads)
                        top = mx[:, s % 2, 0:heads]
                        dve.wait_ge(s_S, NUB * b + s + 1)
                        chain(dve, nc.vector.tensor_reduce(top, sc, AX.X, ALU.max), base)
                        nc.vector.tensor_tensor(prob[:, s % RING, :].rearrange("p (h k) -> p h k", h=heads), sc,
                                                top.unsqueeze(2).to_broadcast([P, heads, 512 // heads]),
                                                ALU.subtract).then_inc(s_shift, 1)
                        for part, steps in ((norm, NORM_AT), (embed, EMBED_AT), (stats, STAT_AT)):
                            if s in steps:
                                part(steps.index(s))
                        if s == POOL_AT:
                            pool_latents()
                        if s == IDX_AT:
                            dve_indices(dve, b + 2)
                    for t in range(TS):
                        back, at_ = divmod(NU * t + OUT_AT, NUB)
                        if s == at_ and (m.old if back else m.new):
                            dve_outputs(dve, b - back, (par + back) % 2, t, base)
                        back, at_ = divmod(NU * t + Y_AT, NUB)
                        if s == at_ and (m.old if back else m.new):
                            dve.wait_ge(s_rs1, TS * (b - back) + t + 1)
                            nc.vector.tensor_scalar(y[:, :], h1[:, t % 2, :], mv1[:, 0:1], rs1[:, :],
                                                    ALU.subtract, ALU.mult).then_inc(s_y, 1)
                    for task in plan[s]:
                        dve_misc(dve, m, task, b, 1 - par, base)

            sequence(0, 0, 0)
            PER = CH["n"]
            sequence(1, 1, 0)
            PER = CH["n"] - PER
            base = CH["n"]
            CH["n"] = 0
            with dve.Fori(1, SEQS // 2) as i:
                sequence(2 * i, 0, 2 * PER * (i - 1) + base)
                sequence(2 * i + 1, 1, 2 * PER * (i - 1) + base)
            assert CH["n"] == 2 * PER, CH["n"]
            base += PER * (SEQS - 2)
            CH["n"] = 0
            sequence(SEQS, 0, base)
            for t in range(TS):
                dve.wait_ge(s_rows[t], 16 * (SEQS + 2))
            dve.wait_ge(s_mD, Misc(SEQS).end("D"))
            nc.vector.memset(mx[:, :, :], 0.0).then_inc(s_fin, GT)
            nc.vector.memset(st0[:, :], 0.0).then_inc(s_free, 2)
            for part, k in DVE_PARTS:
                dve_choice(dve, 0, part, k, base)
            dve_stats(dve, 0, 0, base)
            dve_scales(dve, 0, base)
            base += CH["n"]
            CH["n"] = 0
            PER2 = 6 * DIGITS + 2 * GR + 23
            with dve.Fori(0, E - 1) as e:
                dve_expert(dve, e, False, PER2 * e + base)
            assert CH["n"] == PER2, CH["n"]
            base += PER2 * (E - 1)
            CH["n"] = 0
            dve_expert(dve, E - 1, True, base)


NAMES = {"x": "x", "tok_table": "L0_tok_tok_table", "pos_table": "L0_tok_pos_table", "seg_table": "L0_tok_seg_table",
         "wq": "L0_attn_wq", "wk": "L0_attn_wk", "wv": "L0_attn_wv", "wgq": "L0_attn_wgq", "wgk": "L0_attn_wgk",
         "wgv": "L0_attn_wgv", "r_out_w": "L0_attn_r_out_w", "gate_local_w": "L0_attn_gate_local_w",
         "gate_remote_w": "L0_attn_gate_remote_w", "w_out": "L0_attn_w_out", "centroids": "L0_ffn_centroids",
         "ln_g": "L0_ffn_ln_g", "ln_b": "L0_ffn_ln_b", "w1": "L0_ffn_w1", "b1": "L0_ffn_b1", "w2": "L0_ffn_w2",
         "b2": "L0_ffn_b2"}


def kernel(**inputs):
    import concourse.bacc as bacc
    from concourse.bass_utils import run_bass_kernel_spmd

    given = {short: np.ascontiguousarray(inputs[name]) for short, name in NAMES.items()}
    seqs, S = given["x"].shape
    E, _, F = given["w1"].shape
    given["tables"], widths, given["digit_table"] = constants(S)

    nc = bacc.Bacc("TRN2", target_bir_lowering=False, num_devices=1)
    arrays, aps = {}, {}
    for name, a in given.items():
        arrays[f"in_{name}"] = a
        aps[name] = nc.dram_tensor(f"in_{name}", a.shape, mybir.dt.from_np(a.dtype), kind="ExternalInput").ap()
    out = nc.dram_tensor("out_rows", [seqs * S, D], F32, kind="ExternalOutput").ap()
    tower(nc, aps, out, aps["tables"], aps["digit_table"], widths, seqs, S, given["tok_table"].shape[0], F, E)
    r = run_bass_kernel_spmd(nc, [arrays], core_ids=[0])
    return np.asarray(r.results[0]["out_rows"]).reshape(seqs, S, D)
```
